# Optimizing a Trainium2 kernel written in Bass

```python
import numpy as np
import jax
import jax.numpy as jnp

def _softmax(x, axis=-1):
    return jax.nn.softmax(x, axis=axis)

def _gelu(x):
    return jax.nn.gelu(x, approximate=True)

def _silu(x):
    return jax.nn.silu(x)

def _sigmoid(x):
    return jax.nn.sigmoid(x)

def _layernorm(x, axis=-1, eps=1e-05):
    m = jnp.mean(x, axis=axis, keepdims=True)
    v = jnp.var(x, axis=axis, keepdims=True)
    return (x - m) / jnp.sqrt(v + eps)

def _scatter_add(tgt, idx, src, axis=0):
    return tgt.at[idx].add(src)

def _segment_sum(src, seg, n):
    return jax.ops.segment_sum(src, seg, n)
kernel_name = 'mk_flamingo_gated_d2_seqx_r2_70449d'

def setup_inputs(seed: int=0):
    np.random.seed(seed)
    _w = jnp.asarray

    def _rec_inputs():
        import jax
        import jax.numpy as jnp
        _rk = jax.random.key(seed)
        x = -0.0005146 + 1 * jax.random.normal(jax.random.fold_in(_rk, 1), (8, 512, 512), jnp.float32)
        _lenS = 512 - jax.random.randint(jax.random.fold_in(_rk, 7), (8,), 0, max(1, 512 // 4) + 1, jnp.int32)
        _lenS2 = 120 - jax.random.randint(jax.random.fold_in(_rk, 8), (8,), 0, max(1, 120 // 4) + 1, jnp.int32)
        _ctx_768P = jax.random.normal(jax.random.fold_in(_rk, 11), (8, 16, 384), jnp.float32)
        _ctx_768c = jax.random.dirichlet(jax.random.fold_in(_rk, 511), 0.3 * jnp.ones((16,), jnp.float32), (8, 120))
        _ctx_768t = jnp.einsum('bsk,bkd->bsd', _ctx_768c, _ctx_768P)
        _ctx_768t = _ctx_768t * jax.lax.rsqrt(jnp.mean(jnp.square(_ctx_768t)) + 1e-12) * 0.953939
        ctx_768 = -0.00040386 + 0.999972 * (_ctx_768t + 0.3 * jax.random.normal(jax.random.fold_in(_rk, 611), (8, 120, 384), jnp.float32))
        _validS = jnp.arange(512)[None, :] < _lenS[:, None]
        _validS2 = jnp.arange(120)[None, :] < _lenS2[:, None]
        _causal = jnp.tril(jnp.ones((512, 512), dtype=bool))
        mask_BxS2_bk0 = jnp.logical_not(jnp.broadcast_to(_validS2[:, :], (8, 120)))
        _g = jax.random.normal(jax.random.fold_in(_rk, 9001), (2, 2), jnp.float32)
        _g = jnp.sign(_g) * jnp.maximum(jnp.abs(_g), 1.0) + (_g == 0) * 1.0
        g_xattn = _g[0]
        g_ffn = _g[1]
        return (x, ctx_768, mask_BxS2_bk0, g_xattn, g_ffn)
    x, ctx_768, mask_BxS2_bk0, g_xattn, g_ffn = _rec_inputs()

    def _L0_xattn_setup():
        import jax, jax.numpy as jnp
        import numpy as np
        DIM_IN, DIM_LAT, DIM_HEAD = (384, 512, 64)
        INNER = max(DIM_LAT, DIM_IN)
        HEADS = INNER // DIM_HEAD
        SCALE = DIM_HEAD ** (-0.5)
        RMS_EPS = 1e-08
        LN_EPS = 1e-05

        def layernorm(x, g, b):
            mu = jnp.mean(x, axis=-1, keepdims=True)
            var = jnp.mean((x - mu) ** 2, axis=-1, keepdims=True)
            return (x - mu) * jax.lax.rsqrt(var + LN_EPS) * g + b

        def rmsnorm(x, gamma):
            norm = jnp.sqrt(jnp.sum(x * x, axis=-1, keepdims=True)) * x.shape[-1] ** (-0.5)
            return x / jnp.maximum(norm, RMS_EPS) * gamma
        key = jax.random.key(seed)
        ks = jax.random.split(key, 12)
        b, n, m = (4, 2048, 256)
        x = jax.random.normal(ks[0], (b, n, DIM_IN), jnp.float32)
        latents = jax.random.normal(ks[1], (b, m, DIM_LAT), jnp.float32)
        mask = jax.random.randint(ks[2], (b, n), 0, 2).astype(bool)
        s = lambda k, sh, fan: jax.random.normal(k, sh, jnp.float32) * fan ** (-0.5)
        return {'x': x, 'latents': latents, 'mask': mask, 'ln_x_g': jnp.ones((DIM_IN,), jnp.float32), 'ln_x_b': jnp.zeros((DIM_IN,), jnp.float32), 'ln_l_g': jnp.ones((DIM_LAT,), jnp.float32), 'ln_l_b': jnp.zeros((DIM_LAT,), jnp.float32), 'qn_g': jnp.ones((DIM_HEAD,), jnp.float32), 'kn_g': jnp.ones((DIM_HEAD,), jnp.float32), 'Wq': s(ks[3], (INNER, DIM_LAT), DIM_LAT), 'Wkv': s(ks[4], (2 * INNER, DIM_IN), DIM_IN), 'Wlkv': s(ks[5], (2 * INNER, DIM_LAT), DIM_LAT), 'Wo': s(ks[6], (DIM_LAT, INNER), INNER), 'bo': jnp.zeros((DIM_LAT,), jnp.float32)}
    _L0_xattn_all = _L0_xattn_setup()
    _L0_xattn_in = {k: v for k, v in _L0_xattn_all.items() if k in ('ln_x_g', 'ln_x_b', 'ln_l_g', 'ln_l_b', 'qn_g', 'kn_g', 'Wq', 'Wkv', 'Wlkv', 'Wo', 'bo')}
    del _L0_xattn_all

    def _L0_ffn_setup():
        import jax, jax.numpy as jnp
        import numpy as np
        SL, BS, HS, FF, E, TOPK = (1024, 2, 512, 2048, 8, 2)
        key = jax.random.key(seed)
        ks = jax.random.split(key, 6)
        T = SL * BS
        x = jax.random.normal(ks[0], (SL, BS, HS), jnp.float32)
        scores = jax.random.uniform(ks[1], (T, E), jnp.float32)
        expert_weights = jax.random.uniform(ks[2], (T, TOPK), jnp.float32)
        expert_indices = jax.random.randint(ks[3], (T, TOPK), 0, E, jnp.int32)
        w1 = jax.random.normal(ks[4], (E, HS, FF), jnp.float32) * (1.0 / np.sqrt(HS))
        w2 = jax.random.normal(ks[5], (E, FF, HS), jnp.float32) * (1.0 / np.sqrt(FF))
        bias = jnp.zeros((HS,), jnp.float32)
        return dict(x=x, scores=scores, expert_weights=expert_weights, expert_indices=expert_indices, w1=w1, w2=w2, bias=bias)
    _L0_ffn_all = _L0_ffn_setup()
    _L0_ffn_in = {k: v for k, v in _L0_ffn_all.items() if k in ('scores', 'expert_weights', 'expert_indices', 'w1', 'w2', 'bias')}
    del _L0_ffn_all

    def _L1_xattn_setup():
        import jax, jax.numpy as jnp
        import numpy as np
        N_HEADS = 16
        D_EMBED = 512
        D_CROSS = 384
        D_HEAD = D_EMBED // N_HEADS
        key = jax.random.key(seed)
        ks = jax.random.split(key, 10)
        B, SQ, SKV = (8, 2048, 77)
        s_e = 1.0 / np.sqrt(D_EMBED)
        s_c = 1.0 / np.sqrt(D_CROSS)
        return {'x': jax.random.normal(ks[0], (B, SQ, D_EMBED), jnp.float32), 'y': jax.random.normal(ks[1], (B, SKV, D_CROSS), jnp.float32), 'wq': jax.random.normal(ks[2], (D_EMBED, D_EMBED), jnp.float32) * s_e, 'bq': jnp.zeros((D_EMBED,), jnp.float32), 'wk': jax.random.normal(ks[3], (D_CROSS, D_EMBED), jnp.float32) * s_c, 'bk': jnp.zeros((D_EMBED,), jnp.float32), 'wv': jax.random.normal(ks[4], (D_CROSS, D_EMBED), jnp.float32) * s_c, 'bv': jnp.zeros((D_EMBED,), jnp.float32), 'wo': jax.random.normal(ks[5], (D_EMBED, D_EMBED), jnp.float32) * s_e, 'bo': jnp.zeros((D_EMBED,), jnp.float32)}
    _L1_xattn_all = _L1_xattn_setup()
    _L1_xattn_in = {k: v for k, v in _L1_xattn_all.items() if k in ('wq', 'bq', 'wk', 'bk', 'wv', 'bv', 'wo', 'bo')}
    del _L1_xattn_all

    def _L1_ffn_setup():
        import jax, jax.numpy as jnp
        import numpy as np
        E, K, D, H = (8, 2, 512, 1024)
        B, S = (1, 512)

        def _grouped_swiglu(x_sorted, counts, w1, w2, w3):
            if hasattr(jax.lax, 'ragged_dot'):
                gs = counts.astype(jnp.int32)
                h = jax.nn.silu(jax.lax.ragged_dot(x_sorted, w1, gs)) * jax.lax.ragged_dot(x_sorted, w3, gs)
                return jax.lax.ragged_dot(h, w2, gs)
            pos = jnp.arange(x_sorted.shape[0])
            eid = jnp.searchsorted(jnp.cumsum(counts), pos, side='right')
            out = jnp.zeros((x_sorted.shape[0], w2.shape[-1]), x_sorted.dtype)
            for e in range(w1.shape[0]):
                xm = jnp.where((eid == e)[:, None], x_sorted, 0.0)
                he = jax.nn.silu(xm @ w1[e]) * (xm @ w3[e])
                out = out + he @ w2[e]
            return out
        key = jax.random.key(seed)
        k0, k1, k2, k3, k4 = jax.random.split(key, 5)
        sD = 1.0 / np.sqrt(D)
        sH = 1.0 / np.sqrt(H)
        return {'hidden_states': jax.random.normal(k0, (B, S, D), jnp.float32), 'gate_w': jax.random.normal(k1, (E, D), jnp.float32) * sD, 'w1': jax.random.normal(k2, (E, D, H), jnp.float32) * sD, 'w2': jax.random.normal(k3, (E, H, D), jnp.float32) * sH, 'w3': jax.random.normal(k4, (E, D, H), jnp.float32) * sD}
    _L1_ffn_all = _L1_ffn_setup()
    _L1_ffn_in = {k: v for k, v in _L1_ffn_all.items() if k in ('gate_w', 'w1', 'w2', 'w3')}
    del _L1_ffn_all
    return {'x': x, 'ctx_768': ctx_768, 'mask_BxS2_bk0': mask_BxS2_bk0, 'g_xattn': g_xattn, 'g_ffn': g_ffn, 'L0_xattn_ln_x_g': _L0_xattn_in['ln_x_g'], 'L0_xattn_ln_x_b': _L0_xattn_in['ln_x_b'], 'L0_xattn_ln_l_g': _L0_xattn_in['ln_l_g'], 'L0_xattn_ln_l_b': _L0_xattn_in['ln_l_b'], 'L0_xattn_qn_g': _L0_xattn_in['qn_g'], 'L0_xattn_kn_g': _L0_xattn_in['kn_g'], 'L0_xattn_Wq': _L0_xattn_in['Wq'], 'L0_xattn_Wkv': _L0_xattn_in['Wkv'], 'L0_xattn_Wlkv': _L0_xattn_in['Wlkv'], 'L0_xattn_Wo': _L0_xattn_in['Wo'], 'L0_xattn_bo': _L0_xattn_in['bo'], 'L0_ffn_scores': _L0_ffn_in['scores'], 'L0_ffn_expert_weights': _L0_ffn_in['expert_weights'], 'L0_ffn_expert_indices': _L0_ffn_in['expert_indices'], 'L0_ffn_w1': _L0_ffn_in['w1'], 'L0_ffn_w2': _L0_ffn_in['w2'], 'L0_ffn_bias': _L0_ffn_in['bias'], 'L1_xattn_wq': _L1_xattn_in['wq'], 'L1_xattn_bq': _L1_xattn_in['bq'], 'L1_xattn_wk': _L1_xattn_in['wk'], 'L1_xattn_bk': _L1_xattn_in['bk'], 'L1_xattn_wv': _L1_xattn_in['wv'], 'L1_xattn_bv': _L1_xattn_in['bv'], 'L1_xattn_wo': _L1_xattn_in['wo'], 'L1_xattn_bo': _L1_xattn_in['bo'], 'L1_ffn_gate_w': _L1_ffn_in['gate_w'], 'L1_ffn_w1': _L1_ffn_in['w1'], 'L1_ffn_w2': _L1_ffn_in['w2'], 'L1_ffn_w3': _L1_ffn_in['w3']}

def reference(x, ctx_768, mask_BxS2_bk0, g_xattn, g_ffn, L0_xattn_ln_x_g, L0_xattn_ln_x_b, L0_xattn_ln_l_g, L0_xattn_ln_l_b, L0_xattn_qn_g, L0_xattn_kn_g, L0_xattn_Wq, L0_xattn_Wkv, L0_xattn_Wlkv, L0_xattn_Wo, L0_xattn_bo, L0_ffn_scores, L0_ffn_expert_weights, L0_ffn_expert_indices, L0_ffn_w1, L0_ffn_w2, L0_ffn_bias, L1_xattn_wq, L1_xattn_bq, L1_xattn_wk, L1_xattn_bk, L1_xattn_wv, L1_xattn_bv, L1_xattn_wo, L1_xattn_bo, L1_ffn_gate_w, L1_ffn_w1, L1_ffn_w2, L1_ffn_w3):
    import jax
    import jax.numpy as jnp

    def _L0_xattn_ref(x, latents, mask, ln_x_g, ln_x_b, ln_l_g, ln_l_b, qn_g, kn_g, Wq, Wkv, Wlkv, Wo, bo):
        import jax, jax.numpy as jnp
        import numpy as np
        DIM_IN, DIM_LAT, DIM_HEAD = (384, 512, 64)
        INNER = max(DIM_LAT, DIM_IN)
        HEADS = INNER // DIM_HEAD
        SCALE = DIM_HEAD ** (-0.5)
        RMS_EPS = 1e-08
        LN_EPS = 1e-05

        def layernorm(x, g, b):
            mu = jnp.mean(x, axis=-1, keepdims=True)
            var = jnp.mean((x - mu) ** 2, axis=-1, keepdims=True)
            return (x - mu) * jax.lax.rsqrt(var + LN_EPS) * g + b

        def rmsnorm(x, gamma):
            norm = jnp.sqrt(jnp.sum(x * x, axis=-1, keepdims=True)) * x.shape[-1] ** (-0.5)
            return x / jnp.maximum(norm, RMS_EPS) * gamma
        b, n, _ = x.shape
        m = latents.shape[1]
        xn = layernorm(x, ln_x_g, ln_x_b)
        ln = layernorm(latents, ln_l_g, ln_l_b)
        q = ln @ Wq.T
        kv = jnp.concatenate([xn @ Wkv.T, ln @ Wlkv.T], axis=1)
        k, v = (kv[..., :INNER], kv[..., INNER:])
        split_heads = lambda t: t.reshape(t.shape[0], t.shape[1], HEADS, DIM_HEAD).transpose(0, 2, 1, 3)
        q, k, v = (split_heads(q), split_heads(k), split_heads(v))
        qn = rmsnorm(q, qn_g) * SCALE
        kn = rmsnorm(k, kn_g)
        attn = jnp.einsum('bhid,bhjd->bhij', qn, kn)
        full_mask = jnp.pad(mask, ((0, 0), (0, m)), constant_values=True)
        attn = jnp.where(full_mask[:, None, None, :], attn, -jnp.finfo(attn.dtype).max)
        attn = jax.nn.softmax(attn, axis=-1)
        out = jnp.einsum('bhij,bhjd->bhid', attn, v)
        out = out.transpose(0, 2, 1, 3).reshape(b, m, INNER)
        return out @ Wo.T + bo

    def _L0_ffn_ref(x, scores, expert_weights, expert_indices, w1, w2, bias):
        import jax, jax.numpy as jnp
        import numpy as np
        SL, BS, HS, FF, E, TOPK = (1024, 2, 512, 2048, 8, 2)
        sl, bs, hs = x.shape
        n_exp = w1.shape[0]
        top_k = expert_indices.shape[-1]
        xf = x.reshape(-1, hs)
        flat_idx = expert_indices.reshape(-1)
        flat_w = expert_weights.reshape(-1)
        order = jnp.argsort(flat_idx)
        tok = order // top_k
        tokens_per_expert = jnp.bincount(flat_idx, length=n_exp).astype(jnp.int32)
        xs = xf[tok]
        h = jax.nn.gelu(jax.lax.ragged_dot(xs, w1, tokens_per_expert), approximate=False)
        ys = jax.lax.ragged_dot(h, w2, tokens_per_expert)
        ys = ys * flat_w[order][:, None]
        out = jnp.zeros_like(xf).at[tok].add(ys)
        return out.reshape(sl, bs, hs) + bias

    def _L1_xattn_ref(x, y, wq, bq, wk, bk, wv, bv, wo, bo):
        import jax, jax.numpy as jnp
        import numpy as np
        N_HEADS = 16
        D_EMBED = 512
        D_CROSS = 384
        D_HEAD = D_EMBED // N_HEADS
        B, SQ, _ = x.shape
        SKV = y.shape[1]
        q = (x @ wq + bq).reshape(B, SQ, N_HEADS, D_HEAD)
        k = (y @ wk + bk).reshape(B, SKV, N_HEADS, D_HEAD)
        v = (y @ wv + bv).reshape(B, SKV, N_HEADS, D_HEAD)
        scores = jnp.einsum('bqhd,bkhd->bhqk', q, k) / jnp.sqrt(jnp.asarray(D_HEAD, x.dtype))
        attn = jax.nn.softmax(scores, axis=-1)
        out = jnp.einsum('bhqk,bkhd->bqhd', attn, v).reshape(B, SQ, D_EMBED)
        return out @ wo + bo

    def _L1_ffn_ref(hidden_states, gate_w, w1, w2, w3):
        import jax, jax.numpy as jnp
        import numpy as np
        E, K, D, H = (8, 2, 512, 1024)
        B, S = (1, 512)

        def _grouped_swiglu(x_sorted, counts, w1, w2, w3):
            if hasattr(jax.lax, 'ragged_dot'):
                gs = counts.astype(jnp.int32)
                h = jax.nn.silu(jax.lax.ragged_dot(x_sorted, w1, gs)) * jax.lax.ragged_dot(x_sorted, w3, gs)
                return jax.lax.ragged_dot(h, w2, gs)
            pos = jnp.arange(x_sorted.shape[0])
            eid = jnp.searchsorted(jnp.cumsum(counts), pos, side='right')
            out = jnp.zeros((x_sorted.shape[0], w2.shape[-1]), x_sorted.dtype)
            for e in range(w1.shape[0]):
                xm = jnp.where((eid == e)[:, None], x_sorted, 0.0)
                he = jax.nn.silu(xm @ w1[e]) * (xm @ w3[e])
                out = out + he @ w2[e]
            return out
        x = hidden_states.reshape(-1, D)
        N = x.shape[0]
        scores = jax.nn.softmax(x @ gate_w.T, axis=-1)
        top_scores, sel = jax.lax.top_k(scores, K)
        sel_flat = sel.T.reshape(-1)
        scores_flat = top_scores.T.reshape(-1)
        order = jnp.argsort(sel_flat, stable=True)
        tok_sorted = order % N
        scores_sorted = scores_flat[order]
        counts = jnp.bincount(sel_flat, length=E)
        x_sorted = x[tok_sorted]
        y = _grouped_swiglu(x_sorted, counts, w1, w2, w3)
        weighted = y * scores_sorted[:, None]
        out = jnp.zeros((N, D), x.dtype).at[tok_sorted].add(weighted)
        return out.reshape(hidden_states.shape)
    x = x + jnp.tanh(g_xattn[0]) * _L0_xattn_ref(ctx_768, _layernorm(x, axis=-1), mask_BxS2_bk0, L0_xattn_ln_x_g, L0_xattn_ln_x_b, L0_xattn_ln_l_g, L0_xattn_ln_l_b, L0_xattn_qn_g, L0_xattn_kn_g, L0_xattn_Wq, L0_xattn_Wkv, L0_xattn_Wlkv, L0_xattn_Wo, L0_xattn_bo)
    x = x + jnp.tanh(g_ffn[0]) * _L0_ffn_ref(_layernorm(x, axis=-1), L0_ffn_scores, L0_ffn_expert_weights, L0_ffn_expert_indices, L0_ffn_w1, L0_ffn_w2, L0_ffn_bias)
    x = x + jnp.tanh(g_xattn[1]) * _L1_xattn_ref(_layernorm(x, axis=-1), ctx_768, L1_xattn_wq, L1_xattn_bq, L1_xattn_wk, L1_xattn_bk, L1_xattn_wv, L1_xattn_bv, L1_xattn_wo, L1_xattn_bo)
    x = x + jnp.tanh(g_ffn[1]) * _L1_ffn_ref(_layernorm(x, axis=-1), L1_ffn_gate_w, L1_ffn_w1, L1_ffn_w2, L1_ffn_w3)
    return x

_drawn_inputs = setup_inputs


def setup_inputs(seed=0):
    import zlib

    import numpy as np

    out = dict(_drawn_inputs(seed))
    spreads = {'g_ffn': (-1.0, 0.6),
     'L0_xattn_ln_x_g': (1.0, 0.6),
     'L0_xattn_ln_x_b': (0.0, 0.8),
     'L0_xattn_ln_l_g': (1.0, 0.574),
     'L0_xattn_ln_l_b': (0.0, 0.1),
     'L0_xattn_qn_g': (1.0, 0.6),
     'L0_xattn_kn_g': (1.0, 0.6),
     'L0_xattn_bo': (0.0, 0.1),
     'L0_ffn_bias': (0.0, 0.1),
     'L1_xattn_bq': (0.0, 0.355),
     'L1_xattn_bk': (0.0, 0.8),
     'L1_xattn_bv': (0.0, 0.1),
     'L1_xattn_bo': (0.0, 0.1)}
    factors = {'L0_xattn_Wkv': 2.895}
    for name, (base, spread) in spreads.items():
        noise = np.random.default_rng([zlib.crc32(name.encode()), seed]).standard_normal(out[name].shape)
        drawn = base * np.exp(spread * noise) if base else spread * noise
        out[name] = jnp.asarray(drawn.astype(out[name].dtype))
    for name, factor in factors.items():
        out[name] = (out[name] * factor).astype(out[name].dtype)
    return out
```

```python
from contextlib import ExitStack

import concourse.bass as bass
from concourse import mybir

F32 = mybir.dt.float32
F32R = mybir.dt.float32r
I32 = mybir.dt.int32
U8 = mybir.dt.uint8
ALU = mybir.AluOpType
ACT = mybir.ActivationFunctionType
AX = mybir.AxisListType

P = 128
D = 512
DC = D // P
B, S = 8, 512
QT = S // P
NTOK = B * S
CL, CD = 120, 384
CC = CD // P
KEYS = S + CL
EPS = 1e-5
E = 8
ROWS = 256
TOK0 = 2048
NA0 = 2 * TOK0 // P
NA1 = 2 * NTOK // P
NT0 = 2 * TOK0 // ROWS + E - 1
NT1 = 2 * NTOK // ROWS + E - 1
FF0, FF1 = 2048, 1024
MASKED = -1e30


class Count:

    def __init__(self, ctx, nc, name, per, credit=0):
        self.sem = ctx.enter_context(nc.semaphore(name))
        self.per, self.credit = per, credit

    def have(self, b, j):
        return b * self.per + (j + 1 + self.credit)

    def back(self, b, j, depth):
        assert self.credit >= depth
        return b * self.per + (j + 1 + self.credit - depth)


def ds(a, n):
    return bass.ds(a, n)


class Semaphores:

    def __init__(self, nc):
        self.nc, self.all = nc, []

    def enter_context(self, made):
        self.all.append(made.__enter__())
        return self.all[-1]

    def give_back(self):
        self.nc.clear_and_free_semaphores(self.all)
        self.nc.all_engine_barrier()


class Core:
    pass


def setup(nc, k, ins):
    with ExitStack() as ctx:
        sem = lambda n: k.sems.enter_context(nc.semaphore(n))
        zeroed, masks, loaded, tanhed = sem("zeroed"), sem("masks"), sem("setup_loaded"), sem("tanhed")
        graw = ctx.enter_context(nc.sbuf_tensor("graw", [P, 4], F32))
        with nc.Block() as block:
            @block.gpsimd
            def _(pool):
                pool.memset(k.ident[:, :], 0.0).then_inc(zeroed, 1)
                pool.memset(k.tri[:, :], 1.0).then_inc(zeroed, 1)
                pool.memset(k.ones[:, :], 1.0)
                pool.memset(k.halfneg[:, :], -0.5)
                pool.iota(k.iota_e[:, :], [[1, E]], base=0, channel_multiplier=0,
                          allow_small_or_imprecise_dtypes=True)
                pool.iota(k.iota_p[:, :], [[1, P]], base=0, channel_multiplier=0,
                          allow_small_or_imprecise_dtypes=True)
                pool.iota(k.tokcol[:, :], [[P, B * QT]], base=0, channel_multiplier=1,
                          allow_small_or_imprecise_dtypes=True)
                pool.wait_ge(zeroed, 2)
                pool.affine_select(out=k.ident[:, :], in_=k.ident[:, :], compare_op=ALU.not_equal, fill=1.0,
                                   base=0, pattern=[[-1, P]], channel_multiplier=1).then_inc(masks, 1)
                pool.affine_select(out=k.tri[:, :], in_=k.tri[:, :], compare_op=ALU.is_gt, fill=0.0,
                                   base=0, pattern=[[1, P]], channel_multiplier=-1).then_inc(masks, 1)
                pool.wait_ge(masks, 2)

            @block.sync
            def _(sp):
                sp.dma_start(graw[:, 0:2], ins["g_xattn"][None, :].to_broadcast([P, 2])).then_inc(loaded, 16)
                sp.dma_start(graw[:, 2:4], ins["g_ffn"][None, :].to_broadcast([P, 2])).then_inc(loaded, 16)

            @block.scalar
            def _(act):
                act.wait_ge(loaded, 32)
                act.activation(k.gate[:, :], graw[:, :], ACT.Tanh).then_inc(tanhed, 1)
                act.wait_ge(tanhed, 1)


LN_PIECES = [("a", 0), ("a", 1), ("b", 0), ("a", 2), ("b", 1), ("c", 0), ("a", 3), ("b", 2), ("c", 1),
             ("a", 4), ("b", 3), ("c", 2), ("c", 3), ("b", 4)]
LN_STATS = [q for q in LN_PIECES if q[0] == "a" or (q[0] == "b" and q[1] < 4)]
H0 = 8
DH0 = D // H0
U0 = H0 * QT
PRING = 4


def attention0(nc, k, ins):
    sems = Semaphores(nc)
    with ExitStack() as ctx:
        sb = lambda n, s, d=F32: ctx.enter_context(nc.sbuf_tensor("a0_" + n, s, d))
        sem = lambda n: sems.enter_context(nc.semaphore("a0_" + n))
        count = lambda n, per, credit=0: Count(sems, nc, "a0_" + n, per, credit)
        wq, wlkv, wkv, wo = sb("wq", [P, DC, D]), sb("wlkv", [P, DC, 2 * D]), sb("wkv", [P, CC, 2 * D]), sb("wo", [P, DC, D])
        lng, lnb, lxg, lxb = sb("lng", [P, DC]), sb("lnb", [P, DC]), sb("lxg", [P, CC]), sb("lxb", [P, CC])
        qg, kg, qgain = sb("qg", [P, 1]), sb("kg", [P, 1]), sb("qgain", [P, 1])
        bog = sb("bog", [P, D])
        mraw, mrow = sb("mraw", [1, B, CL], U8), sb("mrow", [1, B, CL], F32R)
        X, XC = sb("X", [P, QT, D]), sb("XC", [P, CD])
        Y, YC = sb("Y", [P, QT, D]), sb("YC", [P, CD])
        bst, mv = sb("bst", [P, 9, 6]), sb("mv", [P, 9, 2])
        veps, rstd = sb("veps", [P, 9]), sb("rstd", [P, 9])
        xT = sb("xT", [P, 2, DC, P])
        sq, ss, sc, rn = sb("sq", [P, 2 * D]), sb("ss", [P, 2 * H0]), sb("sc", [P, 2 * H0]), sb("rn", [P, 2 * H0])
        qkn = sb("qkn", [P, 2, 2 * D])
        Q2, KH, KL = sb("Q2", [P, H0, S], F32R), sb("KH", [P, H0, KEYS], F32R), sb("KL", [P, H0, KEYS], F32R)
        V = sb("V", [P, QT + 1, D])
        one_row = sb("one_row", [1, P], F32R)
        Pr, PT = sb("Pr", [P, PRING, KEYS]), sb("PT", [P, 2, QT + 1, S])
        nmax, rsum, rinv = sb("nmax", [P, 4]), sb("rsum", [P, 4]), sb("rinv", [P, 4])
        OT, R = sb("OT", [P, DC, S]), sb("R", [P, QT, D])
        bank = k.bank
        trb = bank[:, 0, :]
        qkbs, vb = [bank[:, 1:3, :], bank[:, 3:5, :]], bank[:, 5, :]
        tqb, tkb = bank[:, 6, :], bank[:, 7, :]
        Sb = [bank[:, 0:2, :].rearrange("p a b -> p (a b)"), bank[:, 2:4, :].rearrange("p a b -> p (a b)")]
        chunks = lambda bk: bk.rearrange("p (c n) -> p c n", c=DC)
        ptm, ptc, otb = [bank[:, 4, :], bank[:, 5, :]], bank[:, 6, :], bank[:, 7, :]

        w_in, folded, folding = sem("weights_in"), sem("folded"), sem("folding")
        n_w_in = 16 * 14
        x_in = [sem(f"x_in{t}") for t in range(QT + 1)]
        r_in = [sem(f"r_in{t}") for t in range(QT)]
        r_stored = [sem(f"r_stored{t}") for t in range(QT)]
        x_free = count("x_free", 5)
        ln_step = count("ln_step", 13)
        stat, rst = count("stat", 9), count("rstd_ready", 9)
        veps_step = count("veps_step", 9)
        y_ready, y_read = count("y_ready", 5), count("y_read", 5, 5)
        xT_ready = count("xT_ready", 5, 2)
        v_done, qk_done = count("v_done", 5), count("qk_done", 5, 2)
        squared, ss_done = count("squared", 5), count("ss_done", 5, 1)
        sc_step, rn_done = count("sc_step", 5), count("rn_done", 5, 1)
        qkn_ready, v_copied = count("qkn_ready", 5, 2), count("v_copied", 5, 1)
        tqk_done = count("tqk_done", 5, 2)
        high_ready, low_ready = count("high_ready", 5), count("low_ready", 5, 1)
        s_done, max_done, exp_done = count("s_done", U0), count("max_done", U0), count("exp_done", U0, 2)
        rinv_step, p_ready, t_done = count("rinv_step", U0), count("p_ready", U0), count("t_done", U0, PRING)
        ptm_out, ptc_out = count("ptm_out", U0, 2), count("ptc_out", H0, 1)
        pv_done, ot_out = count("pv_done", H0 // 2, 1), count("ot_out", H0 // 2, 1)
        wo_done, r_biased, x1_ready = count("wo_done", QT), count("r_biased", QT), count("x1_ready", QT, QT)

        def rounds(eng, body):
            with eng.Fori(0, B - 1) as b:
                body(b, True)
            body(B - 1, False)

        def credit(eng, *counts):
            for c in counts:
                eng.sem_inc(c.sem, c.credit)

        with nc.Block() as block:
            @block.sync
            def _(sp):
                for dst, src in ((wq, "wqT"), (wlkv, "wlkvT"), (wkv, "wkvT"), (wo, "woT")):
                    sp.dma_start(dst[:, :, :], ins[src].rearrange("(c p) n -> p c n", p=P)).then_inc(w_in, 16)
                for dst, src in ((lng, "lng"), (lnb, "lnb"), (lxg, "lxg"), (lxb, "lxb")):
                    sp.dma_start(dst[:, :], ins[src]).then_inc(w_in, 16)
                for dst, src in ((qg, "qng"), (kg, "kng")):
                    for r in range(2):
                        sp.dma_start(dst[64 * r:64 * r + 64, :], ins[src][:, None]).then_inc(w_in, 16)
                sp.dma_start(bog[:, :], ins["bo0"][None, :].to_broadcast([P, D])).then_inc(w_in, 16)
                sp.dma_start(mraw[:, :, :], ins["mask"][None, :, :]).then_inc(w_in, 16)

                def load_x(b):
                    for t in range(QT):
                        sp.dma_start(X[:, t, :], ins["x"][ds(b * S + t * P, P), :]).then_inc(x_in[t], 16)
                    sp.dma_start(XC[0:CL, :], ins["ctx"][ds(b * CL, CL), :]).then_inc(x_in[QT], 16)

                load_x(0)

                def body(b, more):
                    if more:
                        sp.wait_ge(x_free.sem, x_free.have(b, QT))
                        load_x(b + 1)
                    for t in range(QT):
                        sp.wait_ge(r_stored[t], b * 16 + 16)
                        sp.dma_start(R[:, t, :], ins["x"][ds(b * S + t * P, P), :]).then_inc(r_in[t], 16)
                    for t in range(QT):
                        sp.wait_ge(x1_ready.sem, x1_ready.have(b, t))
                        sp.dma_start(k.x1[ds(b * S + t * P, P), :], R[:, t, :]).then_inc(r_stored[t], 16)

                rounds(sp, body)
                for t in range(QT):
                    sp.wait_ge(r_stored[t], 16 * (B + 1))

            @block.gpsimd
            def _(pool):
                for t in range(QT):
                    pool.sem_inc(r_stored[t], 16)
                credit(pool, rn_done)
                pool.wait_ge(w_in, n_w_in)
                pool.tensor_scalar(bog[:, :], bog[:, :], k.gate[:, 0:1], None, ALU.mult).then_inc(folded, 1)
                pool.tensor_tensor(qgain[:, :], qg[:, :], kg[:, :], ALU.mult).then_inc(folding, 1)
                pool.tensor_copy(one_row[:, :], k.ones[0:1, :]).then_inc(folding, 1)
                pool.wait_ge(folding, 2)
                pool.tensor_scalar(qgain[:, :], qgain[:, :], DH0 ** -0.5, None, ALU.mult).then_inc(folded, 1)
                pool.tensor_scalar(mrow[:, :, :], mraw[:, :, :], 1.0, -MASKED, ALU.subtract, ALU.mult).then_inc(folded, 1)
                pool.wait_ge(folded, 3)

                def rstds(b):
                    for n, (kind, t) in enumerate(LN_STATS):
                        rows = CL if t == QT else P
                        pool.wait_ge(stat.sem, stat.have(b, n))
                        pool.nop(nofuse=True)
                        pool.tensor_scalar(veps[0:rows, n:n + 1], mv[0:rows, n, 1:2], EPS, None, ALU.add)\
                            .then_inc(veps_step.sem, 1)
                        pool.wait_ge(veps_step.sem, veps_step.have(b, n))
                        pool.tensor_tensor(rstd[0:rows, n:n + 1], veps[0:rows, n:n + 1], k.halfneg[0:rows, 0:1],
                                           ALU.pow).then_inc(rst.sem, 1)

                rstds(0)

                def body(b, more):
                    for t in range(QT + 1):
                        rows, c0 = (CL, H0) if t == QT else (P, 0)
                        pool.wait_ge(ss_done.sem, ss_done.have(b, t))
                        pool.nop(nofuse=True)
                        pool.tensor_scalar(sc[0:rows, c0:], ss[0:rows, c0:], 1.0 / DH0, 1e-16, ALU.mult, ALU.max)\
                            .then_inc(sc_step.sem, 1)
                        pool.wait_ge(sc_step.sem, sc_step.have(b, t))
                        pool.wait_ge(qkn_ready.sem, qkn_ready.back(b, t, 1))
                        pool.tensor_tensor(rn[0:rows, c0:], sc[0:rows, c0:], k.halfneg[0:rows, c0:],
                                           ALU.pow).then_inc(rn_done.sem, 1)
                    for t in range(QT):
                        pool.wait_ge(r_in[t], b * 16 + 16)
                        pool.tensor_tensor(R[:, t, :], R[:, t, :], bog[:, :], ALU.add).then_inc(r_biased.sem, 1)
                    if more:
                        rstds(b + 1)

                rounds(pool, body)

            @block.tensor
            def _(pe):
                credit(pe, y_read, qk_done, tqk_done, t_done, pv_done)
                pe.wait_ge(folded, 3)

                def body(b, more):
                    def tr(t):
                        rows, ch, src = (CL, CC, YC[0:CL, :]) if t == QT else (P, DC, Y[:, t, :])
                        pe.wait_ge(y_ready.sem, y_ready.have(b, t))
                        pe.wait_ge(xT_ready.sem, xT_ready.back(b, t, 1))
                        for c in range(ch):
                            mm = nc.tensor.transpose(trb[:, c * P:c * P + rows], src[:, c * P:c * P + P],
                                                     k.ident[0:rows, 0:rows])
                        mm.then_inc(y_read.sem, 1)

                    def proj(t):
                        rows, ch, kv = (CL, CC, wkv) if t == QT else (P, DC, wlkv)
                        pe.wait_ge(xT_ready.sem, xT_ready.have(b, t))
                        pe.wait_ge(v_copied.sem, v_copied.back(b, t, 1))
                        for c in range(ch):
                            mm = nc.tensor.matmul(vb[0:rows, :], xT[:, t % 2, c, 0:rows], kv[:, c, D:2 * D],
                                                  start=(c == 0), stop=(c == ch - 1))
                        mm.then_inc(v_done.sem, 1)
                        pe.wait_ge(qkn_ready.sem, qkn_ready.back(b, t, 2))
                        qkb = qkbs[t % 2]
                        if t < QT:
                            for c in range(ch):
                                nc.tensor.matmul(qkb[:, 0, :], xT[:, t % 2, c, :], wq[:, c, :],
                                                 start=(c == 0), stop=(c == ch - 1))
                        for c in range(ch):
                            mm = nc.tensor.matmul(qkb[0:rows, 1, :], xT[:, t % 2, c, 0:rows], kv[:, c, 0:D],
                                                  start=(c == 0), stop=(c == ch - 1))
                        mm.then_inc(qk_done.sem, 1)

                    def trqk(t):
                        rows = CL if t == QT else P
                        pe.wait_ge(qkn_ready.sem, qkn_ready.have(b, t))
                        pe.wait_ge(low_ready.sem, low_ready.back(b, t, 1))
                        if t < QT:
                            for c in range(DC):
                                nc.tensor.transpose(tqb[:, c * P:c * P + P], qkn[:, t % 2, c * P:c * P + P], k.ident[:, :])
                        for c in range(DC):
                            mm = nc.tensor.transpose(tkb[:, c * P:c * P + rows],
                                                     qkn[0:rows, t % 2, D + c * P:D + c * P + P], k.ident[0:rows, 0:rows])
                        mm.then_inc(tqk_done.sem, 1)

                    pe.wait_ge(x1_ready.sem, x1_ready.back(b, QT - 1, QT))
                    for s in range(QT + 3):
                        if s <= QT:
                            tr(s)
                        if 1 <= s <= QT + 1:
                            proj(s - 1)
                        if s >= 2:
                            trqk(s - 2)
                    pe.wait_ge(low_ready.sem, low_ready.have(b, QT))
                    pe.wait_ge(v_copied.sem, v_copied.have(b, QT))

                    def scores(n):
                        h, qt = n // QT, n % QT
                        pe.wait_ge(exp_done.sem, exp_done.back(b, n, 2))
                        q = Q2[:, h, qt * P:qt * P + P]
                        for a, z in ((0, S), (S, KEYS)):
                            nc.tensor.matmul(Sb[n % 2][:, a:z], q, KH[:, h, a:z], start=True, stop=False)
                            nc.tensor.matmul(Sb[n % 2][:, a:z], q, KL[:, h, a:z], start=False, stop=(a == 0))
                        nc.tensor.matmul(Sb[n % 2][:, S:KEYS], one_row[:, :], mrow[0:1, ds(b, 1), :]
                                         .rearrange("o a n -> o (a n)"), start=False, stop=True).then_inc(s_done.sem, 1)

                    def turn(n):
                        h, qt = n // QT, n % QT
                        pe.wait_ge(p_ready.sem, p_ready.have(b, n))
                        pe.wait_ge(ptm_out.sem, ptm_out.back(b, n, 2))
                        if qt == 0:
                            pe.wait_ge(ptc_out.sem, ptc_out.back(b, h, 1))
                        for c in range(QT):
                            nc.tensor.transpose(ptm[n % 2][:, c * P:c * P + P], Pr[:, n % PRING, c * P:c * P + P],
                                                k.ident[:, :])
                        nc.tensor.transpose(ptc[0:CL, qt * P:qt * P + P], Pr[:, n % PRING, S:KEYS], k.ident[:, :])\
                            .then_inc(t_done.sem, 1)

                    def pv(g):
                        pe.wait_ge(ptm_out.sem, ptm_out.have(b, 2 * QT * g + 2 * QT - 1))
                        pe.wait_ge(ptc_out.sem, ptc_out.have(b, 2 * g + 1))
                        pe.wait_ge(ot_out.sem, ot_out.back(b, g, 1))
                        for c in range(QT + 1):
                            rows = CL if c == QT else P
                            for r in range(2):
                                h = 2 * g + r
                                mm = nc.tensor.matmul(otb[DH0 * r:DH0 * r + DH0, :], V[0:rows, c, DH0 * h:DH0 * h + DH0],
                                                      PT[0:rows, r, c, :], start=(c == 0), stop=(c == QT))
                        mm.then_inc(pv_done.sem, 1)

                    for n in range(U0 + 3):
                        if n < U0:
                            scores(n)
                        if n >= 10 and (n - 10) % 8 == 0:
                            pv((n - 10) // 8)
                        if 2 <= n < U0 + 2:
                            turn(n - 2)
                    pe.wait_ge(ot_out.sem, ot_out.have(b, 3))
                    for qt in range(QT):
                        for c in range(DC):
                            mm = nc.tensor.matmul(bank[:, qt, :], OT[:, c, qt * P:qt * P + P], wo[:, c, :],
                                                  start=(c == 0), stop=(c == DC - 1))
                        mm.then_inc(wo_done.sem, 1)

                rounds(pe, body)

            @block.scalar
            def _(act):
                credit(act, xT_ready, v_copied, exp_done, ptm_out, ot_out)
                act.wait_ge(folded, 3)

                def body(b, more):
                    for s in range(QT + 3):
                        if s <= QT:
                            t = s
                            rows, ch, g_, b_ = (CL, CC, lxg, lxb) if t == QT else (P, DC, lng, lnb)
                            act.wait_ge(y_read.sem, y_read.have(b, t))
                            act.wait_ge(qk_done.sem, qk_done.back(b, t, 2))
                            for c in range(ch):
                                i = act.activation(xT[:, t % 2, c, 0:rows], trb[:, c * P:c * P + rows],
                                                   ACT.Identity, bias=b_[:, c:c + 1], scale=g_[:, c:c + 1])
                            i.then_inc(xT_ready.sem, 1)
                        if 1 <= s <= QT + 1:
                            t = s - 1
                            rows, c0 = (CL, D) if t == QT else (P, 0)
                            act.wait_ge(v_done.sem, v_done.have(b, t))
                            act.activation(V[0:rows, t, :], vb[0:rows, :], ACT.Copy).then_inc(v_copied.sem, 1)
                            act.wait_ge(qk_done.sem, qk_done.have(b, t))
                            act.wait_ge(ss_done.sem, ss_done.back(b, t, 1))
                            act.activation(sq[0:rows, c0:], qkbs[t % 2][0:rows, :, :].rearrange("p a n -> p (a n)")[:, c0:],
                                           ACT.Square).then_inc(squared.sem, 1)
                        if s >= 2:
                            t = s - 2
                            rows = CL if t == QT else P
                            act.wait_ge(tqk_done.sem, tqk_done.have(b, t))
                            for par in range(2):
                                own, other = slice(DH0 * par, DH0 * par + DH0), slice(DH0 - DH0 * par, P - DH0 * par)
                                if t < QT:
                                    act.activation(Q2[own, par::2, t * P:t * P + P], chunks(tqb)[own, :, :], ACT.Copy,
                                                   scale=qgain[own, 0:1])
                                for to in (own, other):
                                    i = act.activation(KH[to, par::2, t * P:t * P + rows], chunks(tkb)[own, :, 0:rows],
                                                       ACT.Copy)
                            i.then_inc(high_ready.sem, 1)

                    for n in range(U0 + 4):
                        if 3 <= n < U0 + 3:
                            m = n - 3
                            h, qt = m // QT, m % QT
                            act.wait_ge(t_done.sem, t_done.have(b, m))
                            if h % 2 == 0 and qt == 0:
                                act.wait_ge(pv_done.sem, pv_done.back(b, h // 2, 1))
                            act.activation(PT[:, h % 2, 0:QT, qt * P:qt * P + P],
                                           ptm[m % 2].rearrange("p (c n) -> p c n", c=QT), ACT.Copy)\
                                .then_inc(ptm_out.sem, 1)
                        if n < U0:
                            act.wait_ge(max_done.sem, max_done.have(b, n))
                            act.wait_ge(t_done.sem, t_done.back(b, n, PRING))
                            act.activation(Pr[:, n % PRING, :], Sb[n % 2][:, 0:KEYS], ACT.Exp,
                                           bias=nmax[:, n % 4:n % 4 + 1],
                                           accum_out=rsum[:, n % 4:n % 4 + 1]).then_inc(exp_done.sem, 1)
                        if n >= 11 and (n - 11) % 8 == 0:
                            g_ = (n - 11) // 8
                            act.wait_ge(pv_done.sem, pv_done.have(b, g_))
                            act.activation(OT[:, g_, :], otb, ACT.Copy).then_inc(ot_out.sem, 1)

                rounds(act, body)

            @block.vector
            def _(dve):
                credit(dve, ss_done, qkn_ready, low_ready, ptc_out, x1_ready)
                dve.wait_ge(folded, 3)

                def ln_piece(b, piece):
                    kind, t = piece
                    rows, x, y = (CL, XC[0:CL, :], YC[0:CL, :]) if t == QT else (P, X[:, t, :], Y[:, t, :])
                    chain = [q for q in LN_PIECES[:LN_PIECES.index(piece)]]
                    step = sum(1 if q[0] == "a" else (2 if q[0] == "b" and q[1] < QT else 0) for q in chain)

                    def stats(src, step):
                        n = LN_STATS.index(piece)
                        dve.bn_stats(bst[0:rows, n, :], src).then_inc(ln_step.sem, 1)
                        dve.wait_ge(ln_step.sem, ln_step.have(b, step))
                        dve.nop(nofuse=True)
                        dve.bn_aggr(mv[0:rows, n, :], bst[0:rows, n, :]).then_inc(stat.sem, 1)

                    def normalise(dst, src, n):
                        dve.wait_ge(rst.sem, rst.have(b, n))
                        return dve.tensor_scalar(dst, src, mv[0:rows, n, 0:1], rstd[0:rows, n:n + 1],
                                                 ALU.subtract, ALU.mult)
                    if kind == "a":
                        dve.wait_ge(x_in[t], b * 16 + 16)
                        stats(x, step)
                    elif kind == "b":
                        dve.wait_ge(y_read.sem, y_read.back(b, t, 5))
                        i = normalise(y, x, LN_STATS.index(("a", t)))
                        if t == QT:
                            i.then_inc(y_ready.sem, 1)
                            dve.wait_ge(y_ready.sem, y_ready.have(b, 4))
                            dve.sem_inc(x_free.sem, 1)
                        else:
                            i.then_inc(ln_step.sem, 1)
                            dve.wait_ge(ln_step.sem, ln_step.have(b, step))
                            dve.sem_inc(x_free.sem, 1)
                            stats(y, step + 1)
                    else:
                        normalise(y, y, LN_STATS.index(("b", t))).then_inc(y_ready.sem, 1)

                for piece in LN_PIECES:
                    ln_piece(0, piece)

                def body(b, more):
                    for s in range(1, QT + 3):
                        if s <= QT + 1:
                            t = s - 1
                            rows, h0 = (CL, H0) if t == QT else (P, 0)
                            dve.wait_ge(squared.sem, squared.have(b, t))
                            dve.wait_ge(rn_done.sem, rn_done.back(b, t, 1))
                            dve.tensor_reduce(ss[0:rows, h0:], sq[0:rows, h0 * DH0:].rearrange("p (h d) -> p h d", d=DH0),
                                              AX.X, ALU.add).then_inc(ss_done.sem, 1)
                            dve.wait_ge(rn_done.sem, rn_done.have(b, t))
                            dve.wait_ge(tqk_done.sem, tqk_done.back(b, t, 2))
                            dve.tensor_tensor(
                                qkn[0:rows, t % 2, h0 * DH0:].rearrange("p (h d) -> p h d", d=DH0),
                                qkbs[t % 2][0:rows, :, :].rearrange("p a n -> p (a n)")[:, h0 * DH0:]
                                .rearrange("p (h d) -> p h d", d=DH0),
                                rn[0:rows, h0:].unsqueeze(2).to_broadcast([rows, 2 * H0 - h0, DH0]), ALU.mult)\
                                .then_inc(qkn_ready.sem, 1)
                        if s >= 2:
                            t = s - 2
                            rows = CL if t == QT else P
                            dve.wait_ge(high_ready.sem, high_ready.have(b, t))
                            for par in range(2):
                                own, other = slice(DH0 * par, DH0 * par + DH0), slice(DH0 - DH0 * par, P - DH0 * par)
                                if t < QT:
                                    cols = slice(t * P, t * P + P)
                                    dve.scalar_tensor_tensor(Q2[other, par::2, cols], chunks(tqb)[own, :, :],
                                                             qgain[own, 0:1], Q2[own, par::2, cols].bitcast(F32),
                                                             ALU.mult, ALU.subtract)
                                cols = slice(t * P, t * P + rows)
                                for to in (own, other):
                                    i = dve.tensor_tensor(KL[to, par::2, cols], chunks(tkb)[own, :, 0:rows],
                                                          KH[own, par::2, cols].bitcast(F32), ALU.subtract)
                            i.then_inc(low_ready.sem, 1)

                    for n in range(U0 + 3):
                        if n >= 6 and (n - 6) % 4 == 0:
                            h = (n - 6) // 4
                            dve.wait_ge(t_done.sem, t_done.have(b, QT * h + 3))
                            dve.wait_ge(pv_done.sem, pv_done.back(b, h // 2, 1))
                            dve.tensor_copy(PT[0:CL, h % 2, QT, :], ptc[0:CL, :]).then_inc(ptc_out.sem, 1)
                        if n < U0:
                            dve.wait_ge(s_done.sem, s_done.have(b, n))
                            dve.tensor_reduce(nmax[:, n % 4:n % 4 + 1], Sb[n % 2][:, 0:KEYS], AX.X, ALU.max, negate=True)\
                                .then_inc(max_done.sem, 1)
                        if 1 <= n <= U0:
                            m = n - 1
                            dve.wait_ge(exp_done.sem, exp_done.have(b, m))
                            dve.reciprocal(rinv[:, m % 4:m % 4 + 1], rsum[:, m % 4:m % 4 + 1]).then_inc(rinv_step.sem, 1)
                            dve.wait_ge(rinv_step.sem, rinv_step.have(b, m))
                            dve.tensor_scalar(Pr[:, m % PRING, :], Pr[:, m % PRING, :], rinv[:, m % 4:m % 4 + 1], None,
                                              ALU.mult).then_inc(p_ready.sem, 1)
                        if more and n % 2 == 0 and n // 2 < len(LN_PIECES):
                            ln_piece(b + 1, LN_PIECES[n // 2])
                    for qt in range(QT):
                        dve.wait_ge(wo_done.sem, wo_done.have(b, qt))
                        dve.wait_ge(r_biased.sem, r_biased.have(b, qt))
                        dve.scalar_tensor_tensor(R[:, qt, :], bank[:, qt, :], k.gate[:, 0:1], R[:, qt, :],
                                                 ALU.mult, ALU.add).then_inc(x1_ready.sem, 1)

                rounds(dve, body)
    sems.give_back()


def route(nc, k, name, onehot, na, nt, slot_i, idx_i, te_i):
    nh = nt * ROWS // P
    with ExitStack() as ctx:
        sb = lambda n, s, d=F32: ctx.enter_context(nc.sbuf_tensor(name + n, s, d))
        sem = lambda n: k.sems.enter_context(nc.semaphore(name + n))
        tot, inc, off = sb("tot", [P, E, na]), sb("inc", [P, E, na]), sb("off", [P, E, na])
        cnt, cnt_i = sb("cnt", [P, E]), sb("cnt_i", [P, E], I32)
        tiles, tinc, base = sb("tiles", [P, E]), sb("tinc", [P, E]), sb("base", [P, E])
        slot, lo_i, hi_i = sb("slot", [P, na]), sb("lo_i", [P, na], I32), sb("hi_i", [P, na], I32)
        lo, hi = sb("lo", [P, na]), sb("hi", [P, na])
        iota_h, te = sb("iota_h", [P, nh]), sb("te", [P, nt])
        RING = 4
        oh_lo, oh_hi = sb("oh_lo", [P, RING, P]), sb("oh_hi", [P, RING, nh])
        one_na = sb("one_na", [P, na])
        pre_b, tot_b = k.bank[:, 0, 0:E * na], k.bank[:, 1, 0:E * na]
        inv_b = k.bank[:, 2, 0:nh]
        step, made, counted = sem("step"), sem("made"), sem("counted")
        built, used, inverted = sem("built"), sem("used"), sem("inverted")

        with nc.Block() as block:
            @block.gpsimd
            def _(pool):
                pool.iota(iota_h[:, :], [[1, nh]], base=0, channel_multiplier=0,
                          allow_small_or_imprecise_dtypes=True).then_inc(made, 1)
                pool.memset(one_na[:, :], 1.0).then_inc(made, 1)
                pool.wait_ge(made, 2)

            @block.tensor
            def _(pe):
                flat = onehot.rearrange("p e a -> p (e a)")
                nc.tensor.matmul(pre_b, k.tri[:, :], flat, start=True, stop=True)
                nc.tensor.matmul(tot_b, k.ones[:, :], flat, start=True, stop=True).then_inc(counted, 1)

                def invert(a, first, last, n0):
                    for q in range(RING):
                        pe.wait_ge(built, n0 + q + 1)
                        nc.tensor.matmul(inv_b, oh_lo[:, q, :], oh_hi[:, q, :], start=(first and q == 0),
                                         stop=(last and q == RING - 1), skip_group_check=True).then_inc(used, 1)
                invert(0, True, False, 0)
                with pe.Fori(1, na // RING - 1) as g:
                    invert(g, False, False, g * RING)
                invert(0, False, True, na - RING)

            @block.vector
            def _(dve):
                n = [0]

                def then(ins):
                    n[0] += 1
                    ins.then_inc(step, 1)
                    dve.wait_ge(step, n[0])

                dve.wait_ge(made, 2)
                dve.wait_ge(counted, 1)
                then(dve.tensor_copy(tot[:, :, :], tot_b.rearrange("p (e a) -> p e a", e=E)))
                for e in range(E):
                    then(dve.tensor_tensor_scan(inc[:, e, :], one_na[:, :], tot[:, e, :], 0.0, ALU.mult, ALU.add))
                then(dve.tensor_scalar(cnt_i[:, :], inc[:, :, na - 1], float(ROWS - 1), None, ALU.add))
                then(dve.tensor_scalar(cnt_i[:, :], cnt_i[:, :], ROWS.bit_length() - 1, None, ALU.logical_shift_right))
                then(dve.tensor_copy(tiles[:, :], cnt_i[:, :]))
                then(dve.tensor_tensor_scan(tinc[:, :], one_na[:, 0:E], tiles[:, :], 0.0, ALU.mult, ALU.add))
                then(dve.tensor_tensor(base[:, :], tinc[:, :], tiles[:, :], ALU.subtract))
                then(dve.tensor_scalar(base[:, :], base[:, :], float(ROWS), None, ALU.mult))
                then(dve.tensor_tensor(off[:, :, :], inc[:, :, :], tot[:, :, :], ALU.subtract))
                then(dve.tensor_tensor(off[:, :, :], off[:, :, :], pre_b.rearrange("p (e a) -> p e a", e=E), ALU.add))
                then(dve.tensor_tensor(off[:, :, :], off[:, :, :], base[:, :].unsqueeze(2).to_broadcast([P, E, na]), ALU.add))
                then(dve.tensor_tensor(off[:, :, :], off[:, :, :], onehot, ALU.mult))
                then(dve.tensor_reduce(slot[:, :], off[:, :, :].rearrange("p e a -> p a e"), AX.X, ALU.add))
                then(dve.tensor_copy(slot_i, slot[:, :]))
                then(dve.tensor_scalar(lo_i[:, :], slot_i, P - 1, None, ALU.bitwise_and))
                then(dve.tensor_scalar(hi_i[:, :], slot_i, P.bit_length() - 1, None, ALU.logical_shift_right))
                then(dve.tensor_copy(lo[:, :], lo_i[:, :]))
                then(dve.tensor_copy(hi[:, :], hi_i[:, :]))
                then(dve.tensor_scalar(te[:, :], iota_h[:, 0:nt], tinc[:, 0:1], None, ALU.is_ge))
                for e in range(1, E):
                    then(dve.scalar_tensor_tensor(te[:, :], iota_h[:, 0:nt], tinc[:, e:e + 1], te[:, :], ALU.is_ge, ALU.add))
                then(dve.tensor_scalar(te[:, :], te[:, :], float(E - 1), None, ALU.min))
                then(dve.tensor_copy(te_i, te[0:1, :]))
                na2 = na // 2

                def pair(a, tok, q):
                    dve.tensor_scalar(oh_lo[:, q, :], k.iota_p[:, :], lo[:, ds(a, 1)], None, ALU.is_equal)
                    dve.tensor_scalar(oh_hi[:, q, :], iota_h[:, :], hi[:, ds(a, 1)], k.tokcol[:, ds(tok, 1)],
                                      ALU.is_equal, ALU.mult).then_inc(built, 1)
                for q in range(RING):
                    pair(q, q, q)
                with dve.Fori(1, na2 // RING) as g:
                    for q in range(RING):
                        dve.wait_ge(used, (g - 1) * RING + q + 1)
                        pair(g * RING + q, g * RING + q, q)
                with dve.Fori(0, na2 // RING) as g:
                    for q in range(RING):
                        dve.wait_ge(used, na2 - RING + g * RING + q + 1)
                        pair(na2 + g * RING + q, g * RING + q, q)
                dve.wait_ge(used, na)
                then(dve.tensor_copy(idx_i, inv_b))


def route_given(nc, k, ins):
    with ExitStack() as ctx:
        sb = lambda n, s, d=F32: ctx.enter_context(nc.sbuf_tensor("rg_" + n, s, d))
        sem = lambda n: k.sems.enter_context(nc.semaphore("rg_" + n))
        ei, ef, oh = sb("ei", [P, NA0], I32), sb("ef", [P, NA0]), sb("oh", [P, E, NA0])
        ew, loaded, step = sb("ew", [P, NA0]), sem("loaded"), sem("step")
        with nc.Block() as block:
            @block.sync
            def _(sp):
                sp.dma_start(ei[:, :], ins["ei"]).then_inc(loaded, 16)
                sp.dma_start(ew[:, :], ins["ew"]).then_inc(loaded, 16)

            @block.vector
            def _(dve):
                dve.wait_ge(loaded, 32)
                dve.tensor_copy(ef[:, :], ei[:, :]).then_inc(step, 1)
                dve.wait_ge(step, 1)
                dve.tensor_tensor(oh[:, :, :], ef[:, :].unsqueeze(1).to_broadcast([P, E, NA0]),
                                  k.iota_e[:, :].unsqueeze(2).to_broadcast([P, E, NA0]), ALU.is_equal).then_inc(step, 1)
                dve.tensor_scalar(k.w0[:, :], ew[:, :], k.gate[:, 2:3], None, ALU.mult).then_inc(step, 1)
                dve.wait_ge(step, 3)
        route(nc, k, "r0_", oh[:, :, :], NA0, NT0, k.slot0[:, :], k.idx0[:, :], k.te0[:, :])


def route_top2(nc, k):
    NT = B * QT
    with ExitStack() as ctx:
        sb = lambda n, s, d=F32: ctx.enter_context(nc.sbuf_tensor("rt_" + n, s, d))
        sem = lambda n: k.sems.enter_context(nc.semaphore("rt_" + n))
        pr, m, r = sb("pr", [P, NT, E]), sb("m", [P, NT]), sb("r", [P, NT])
        rank, cand, c1, oh = sb("rank", [P, E]), sb("cand", [P, NT, E]), sb("c1", [P, NT]), sb("oh", [P, E, NA1])
        top = sb("top", [P, NA1])
        step, expd = sem("step"), sem("expd")
        centred = sem("centred")
        wide = lambda v: v.unsqueeze(2).to_broadcast([P, NT, E])
        with nc.Block() as block:
            @block.scalar
            def _(act):
                act.wait_ge(centred, 1)
                act.activation(pr[:, :, :], pr[:, :, :], ACT.Exp).then_inc(expd, 1)

            @block.vector
            def _(dve):
                n = [0]

                def then(ins):
                    n[0] += 1
                    ins.then_inc(step, 1)
                    dve.wait_ge(step, n[0])

                then(dve.tensor_reduce(m[:, :], k.logits[:, :, :], AX.X, ALU.max))
                dve.tensor_tensor(pr[:, :, :], k.logits[:, :, :], wide(m[:, :]), ALU.subtract).then_inc(centred, 1)
                then(dve.tensor_scalar(rank[:, :], k.iota_e[:, :], -1.0, float(E), ALU.mult, ALU.add))
                dve.wait_ge(expd, 1)
                then(dve.tensor_reduce(m[:, :], pr[:, :, :], AX.X, ALU.add))
                then(dve.reciprocal(r[:, :], m[:, :]))
                then(dve.tensor_tensor(pr[:, :, :], pr[:, :, :], wide(r[:, :]), ALU.mult))
                for c in range(2):
                    t = top[:, c * NT:c * NT + NT]
                    hot = oh[:, :, c * NT:c * NT + NT].rearrange("p e t -> p t e")
                    rk = rank[:, :].unsqueeze(1).to_broadcast([P, NT, E])
                    then(dve.tensor_reduce(t, pr[:, :, :], AX.X, ALU.max))
                    then(dve.tensor_tensor(cand[:, :, :], pr[:, :, :], wide(t), ALU.is_equal))
                    then(dve.tensor_tensor(cand[:, :, :], cand[:, :, :], rk, ALU.mult))
                    then(dve.tensor_reduce(c1[:, :], cand[:, :, :], AX.X, ALU.max))
                    then(dve.tensor_tensor(cand[:, :, :], rk, wide(c1[:, :]), ALU.is_equal))
                    then(dve.tensor_copy(hot, cand[:, :, :]))
                    if c == 0:
                        then(dve.scalar_tensor_tensor(pr[:, :, :], cand[:, :, :], -2.0, pr[:, :, :], ALU.mult, ALU.add))
                then(dve.tensor_scalar(k.w1[:, :], top[:, :], k.gate[:, 3:4], None, ALU.mult))
        route(nc, k, "r1_", oh[:, :, :], NA1, NT1, k.slot1[:, :], k.idx1[:, :], k.te1[:, :])


def experts(nc, k, name, src, w_up, w_gate, w_down, ff, nt, idx_i, te_i, dst):
    MT = ROWS // P
    FC = ff // P
    SLOTS = 8
    gated = w_gate is not None
    assert SLOTS * (1 if gated else 2) == FC
    with ExitStack() as ctx:
        sb = lambda n, s, d=F32: ctx.enter_context(nc.sbuf_tensor(name + n, s, d))
        sem = lambda n: k.sems.enter_context(nc.semaphore(name + n))
        count = lambda n, per, credit=0: Count(k.sems, nc, name + n, per, credit)
        wu = [sb(f"wu{s}", [P, DC, ff]) for s in range(2)]
        wg = [sb(f"wg{s}", [P, DC, ff]) for s in range(2)] if gated else None
        wd = [sb(f"wd{s}", [P, FC, D]) for s in range(2)]
        X, xT, hT = sb("X", [P, 2, MT, D]), sb("xT", [P, 2, DC, ROWS]), sb("hT", [P, FC, ROWS])
        sil = sb("sil", [P, 2, ROWS])
        Yo = sb("Yo", [P, 2, MT, D])
        icol = sb("icol", [P, 2, MT], I32)
        bst, mv = sb("bst", [P, 2, MT, 6]), sb("mv", [P, 2, MT, 2])
        veps, rstd = sb("veps", [P, 2, MT]), sb("rstd", [P, 2, MT])
        up = [k.bank[:, 0, :], k.bank[:, 1, :]]
        down = [[k.bank[:, 2, :], k.bank[:, 3, :]], [k.bank[:, 4, :], k.bank[:, 5, :]]]
        trb = [k.bank[:, 6, :], k.bank[:, 7, :]]
        te_in = sem("te_seen")
        wu_in, wd_in = [sem(f"wu_in{s}") for s in range(2)], [sem(f"wd_in{s}") for s in range(2)]
        n_up = 32 if gated else 16
        x_in = [[sem(f"x_in{s}{m}") for m in range(MT)] for s in range(2)]
        y_out = [sem(f"y_out{s}") for s in range(2)]
        icopied = count("icopied", 1)
        stepped, stat, rst = count("bn_step", MT), count("stat", MT), count("rstd_ready", 1)
        veps_step = count("veps_step", 1)
        x_ready, x_read = count("x_ready", MT), count("x_read", MT, 2 * MT)
        xT_ready = count("xT_ready", MT, MT)
        up_done, h_ready = count("up_done", SLOTS), count("h_ready", SLOTS, 2)
        sil_done = count("sil_done", SLOTS)
        down_done, y_ready = count("down_done", MT, MT), count("y_ready", MT, 2 * MT)

        def tiles(eng, body):
            assert nt % 2 == 1
            with eng.Fori(0, nt // 2) as i:
                body(2 * i, 0, i, True)
                body(2 * i + 1, 1, i, True)
            body(nt - 1, 0, nt // 2, False)

        with nc.Block() as block:
            @block.sync
            def _(sp):
                def load_up(j, s):
                    e = sp.value_load(te_i[0:1, ds(j, 1)], min_val=0, max_val=E - 1)
                    sp.dma_start(wu[s][:, :, :], w_up[ds(e, 1), :, :].rearrange("o (c p) n -> p (o c) n", p=P))\
                        .then_inc(wu_in[s], 16)
                    if gated:
                        sp.dma_start(wg[s][:, :, :], w_gate[ds(e, 1), :, :].rearrange("o (c p) n -> p (o c) n", p=P))\
                            .then_inc(wu_in[s], 16)

                def load_down(j, s):
                    e = sp.value_load(te_i[0:1, ds(j, 1)], min_val=0, max_val=E - 1)
                    sp.dma_start(wd[s][:, :, :], w_down[ds(e, 1), :, :].rearrange("o (c p) n -> p (o c) n", p=P))\
                        .then_inc(wd_in[s], 16)

                for s in range(2):
                    load_up(s, s)
                    load_down(s, s)

                def step(j, s, i, last):
                    sp.wait_ge(up_done.sem, up_done.have(j, SLOTS - 1))
                    sp.nop(nofuse=True)
                    load_up(j + 2, s)
                    sp.wait_ge(down_done.sem, down_done.have(j, MT - 1))
                    sp.nop(nofuse=True)
                    load_down(j + 2, s)

                with sp.Fori(0, nt // 2 - 1) as i:
                    step(2 * i, 0, i, False)
                    step(2 * i + 1, 1, i, False)
                step(nt - 3, 0, nt // 2 - 1, False)

            @block.gpsimd
            def _(pool):
                def gather(j, s):
                    pool.wait_ge(x_read.sem, x_read.back(j, MT - 1, 2 * MT))
                    pool.tensor_copy(icol[:, s, :], idx_i[:, ds(j * MT, MT)]).then_inc(icopied.sem, 1)
                    pool.wait_ge(icopied.sem, icopied.have(j, 0))
                    pool.nop(nofuse=True)
                    for m in range(MT):
                        pool.indirect_dma_start(X[:, s, m, :], None, src, bass.IndirectOffsetOnAxis(icol[:, s, m:m + 1], 0))\
                            .then_inc(x_in[s][m], 16)

                def rstds(j, s):
                    pool.wait_ge(stat.sem, stat.have(j, MT - 1))
                    pool.nop(nofuse=True)
                    pool.tensor_scalar(veps[:, s, :], mv[:, s, :, 1], EPS, None, ALU.add).then_inc(veps_step.sem, 1)
                    pool.wait_ge(veps_step.sem, veps_step.have(j, 0))
                    pool.tensor_tensor(rstd[:, s, :], veps[:, s, :], k.halfneg[:, 0:MT], ALU.pow).then_inc(rst.sem, 1)

                gather(0, 0)
                gather(1, 1)
                rstds(0, 0)

                with pool.Fori(0, nt // 2 - 1) as i:
                    rstds(2 * i + 1, 1)
                    gather(2 * i + 2, 0)
                    rstds(2 * i + 2, 0)
                    gather(2 * i + 3, 1)
                rstds(nt - 2, 1)
                gather(nt - 1, 0)
                rstds(nt - 1, 0)

            @block.tensor
            def _(pe):
                for c in (x_read, down_done):
                    pe.sem_inc(c.sem, c.credit)

                def turn(j, s):
                    for m in range(MT):
                        pe.wait_ge(x_ready.sem, x_ready.have(j, m))
                        pe.wait_ge(xT_ready.sem, xT_ready.back(j, m, MT))
                        for c in range(DC):
                            mm = nc.tensor.transpose(trb[m][:, c * P:c * P + P], X[:, s, m, c * P:c * P + P], k.ident[:, :])
                        mm.then_inc(x_read.sem, 1)

                turn(0, 0)

                def body(j, s, i, more):
                    pe.wait_ge(wu_in[s], i * n_up + n_up)
                    pe.wait_ge(xT_ready.sem, xT_ready.have(j, MT - 1))
                    for n in range(SLOTS):
                        pe.wait_ge(h_ready.sem, h_ready.back(j, n, 2))
                        for q in range(2):
                            w, f = ((wu, wg)[q], n) if gated else (wu, 2 * n + q)
                            for c in range(DC):
                                mm = nc.tensor.matmul(up[n % 2][:, q * ROWS:q * ROWS + ROWS],
                                                      w[s][:, c, f * P:f * P + P], xT[:, s, c, :],
                                                      start=(c == 0), stop=(c == DC - 1))
                        mm.then_inc(up_done.sem, 1)
                    if more:
                        turn(j + 1, 1 - s)
                    pe.wait_ge(wd_in[s], i * 16 + 16)
                    pe.wait_ge(h_ready.sem, h_ready.have(j, SLOTS - 1))
                    for m in range(MT):
                        pe.wait_ge(y_ready.sem, y_ready.back(j, m, 2 * MT))
                        for f in range(FC):
                            mm = nc.tensor.matmul(down[s][m], hT[:, f, m * P:m * P + P], wd[s][:, f, :],
                                                  start=(f == 0), stop=(f == FC - 1))
                        mm.then_inc(down_done.sem, 1)
                tiles(pe, body)

            @block.scalar
            def _(act):
                act.sem_inc(y_ready.sem, y_ready.credit)
                if not gated:
                    act.sem_inc(h_ready.sem, h_ready.credit)

                def body(j, s, i, more):
                    act.wait_ge(down_done.sem, down_done.back(j, MT - 1, MT))
                    for n in range(SLOTS):
                        act.wait_ge(up_done.sem, up_done.have(j, n))
                        if gated:
                            act.wait_ge(h_ready.sem, h_ready.back(j, n, 2))
                            act.activation(sil[:, n % 2, :], up[n % 2][:, 0:ROWS], ACT.Silu).then_inc(sil_done.sem, 1)
                        else:
                            act.activation(hT[:, 2 * n:2 * n + 2, :], up[n % 2].rearrange("p (q n) -> p q n", q=2), ACT.Gelu)\
                                .then_inc(h_ready.sem, 1)
                    for m in range(MT):
                        if m == 0:
                            act.wait_ge(y_out[s], i * 16 + 16)
                        act.wait_ge(down_done.sem, down_done.have(j, m))
                        act.activation(Yo[:, s, m, :], down[s][m], ACT.Copy).then_inc(y_ready.sem, 1)
                    act.wait_ge(y_ready.sem, y_ready.have(j, MT - 1))
                    act.dma_start(dst[ds(j * ROWS, ROWS), :].rearrange("(m p) n -> p m n", p=P), Yo[:, s, :, :])\
                        .then_inc(y_out[s], 16)
                for s in range(2):
                    act.sem_inc(y_out[s], 16)
                tiles(act, body)
                act.wait_ge(y_out[0], 16 * (nt // 2 + 2))
                act.wait_ge(y_out[1], 16 * (nt // 2 + 1))

            @block.vector
            def _(dve):
                dve.sem_inc(xT_ready.sem, xT_ready.credit)
                if gated:
                    dve.sem_inc(h_ready.sem, h_ready.credit)

                def norm(j, s, i):
                    for m in range(MT):
                        dve.wait_ge(x_in[s][m], i * 16 + 16)
                        dve.bn_stats(bst[:, s, m, :], X[:, s, m, :]).then_inc(stepped.sem, 1)
                    for m in range(MT):
                        dve.wait_ge(stepped.sem, stepped.have(j, m))
                        dve.nop(nofuse=True)
                        dve.bn_aggr(mv[:, s, m, :], bst[:, s, m, :]).then_inc(stat.sem, 1)
                    dve.wait_ge(rst.sem, rst.have(j, 0))
                    for m in range(MT):
                        dve.tensor_scalar(X[:, s, m, :], X[:, s, m, :], mv[:, s, m, 0:1], rstd[:, s, m:m + 1],
                                          ALU.subtract, ALU.mult).then_inc(x_ready.sem, 1)

                def columns(j, s):
                    for m in range(MT):
                        dve.wait_ge(x_read.sem, x_read.have(j, m))
                        dve.tensor_copy(xT[:, s, :, m * P:m * P + P], trb[m].rearrange("p (c n) -> p c n", c=DC))\
                            .then_inc(xT_ready.sem, 1)

                norm(0, 0, 0)
                columns(0, 0)

                def body(j, s, i, more):
                    if more and s == 0:
                        norm(j + 1, 1, i)
                    if more and s == 1:
                        norm(j + 1, 0, i + 1)
                    if gated:
                        dve.wait_ge(down_done.sem, down_done.back(j, MT - 1, MT))
                        for n in range(SLOTS):
                            dve.wait_ge(sil_done.sem, sil_done.have(j, n))
                            dve.tensor_tensor(hT[:, n, :], up[n % 2][:, ROWS:2 * ROWS], sil[:, n % 2, :], ALU.mult)\
                                .then_inc(h_ready.sem, 1)
                    if more:
                        columns(j + 1, 1 - s)
                tiles(dve, body)


H1 = 16
DH1 = D // H1
HH = H1 // 2
U1 = 2 * QT


def attention1(nc, k, ins):
    with ExitStack() as ctx:
        sb = lambda n, s, d=F32: ctx.enter_context(nc.sbuf_tensor("a1_" + n, s, d))
        sem = lambda n: k.sems.enter_context(nc.semaphore("a1_" + n))
        count = lambda n, per, credit=0: Count(k.sems, nc, "a1_" + n, per, credit)
        wq, wk, wv, wo = sb("wq", [P, DC, D]), sb("wk", [P, CC, D]), sb("wv", [P, CC, D]), sb("wo", [P, DC, D])
        gw, ctxT = sb("gw", [P, DC, E]), sb("ctxT", [P, CC, B * CL])
        bq, bk = sb("bq", [P, DC]), sb("bk", [P, DC])
        bv, bo, bf = sb("bv", [P, D]), sb("bo", [P, D]), sb("bf", [P, D])
        kT, V = sb("kT", [P, DC, B * CL]), sb("V", [CL, B, H1, DH1 + 1])
        X, Y = sb("X", [P, QT, D]), sb("Y", [P, QT, D])
        G = sb("G", [P, 2, 2, D])
        icol, wcol = sb("icol", [P, 2, 2], I32), sb("wcol", [P, 2, 2])
        bst, mv = sb("bst", [P, QT, 6]), sb("mv", [P, QT, 2])
        veps, rstd = sb("veps", [P, QT]), sb("rstd", [P, QT])
        xT, qT = sb("xT", [P, DC, S]), sb("qT", [P, DC, S])
        Pr, PT = sb("Pr", [P, 2, HH, CL]), sb("PT", [CL, 2, HH, P])
        smax, rinv = sb("smax", [P, 2, HH]), sb("rinv", [P, 2, HH])
        O, OT = sb("O", [P, 2, D]), sb("OT", [P, 2, DC, P])
        R, N3, N3T = sb("R", [P, QT, D]), sb("N3", [P, 2, D]), sb("N3T", [P, 2, DC, P])
        bst3, mv3 = sb("bst3", [P, QT, 6]), sb("mv3", [P, QT, 2])
        veps3, rstd3 = sb("veps3", [P, QT]), sb("rstd3", [P, QT])
        bank = k.bank
        Sb = [bank[:, 2 * s:2 * s + 2, 0:4 * CL].rearrange("p r (c n) -> p r c n", c=4) for s in range(2)]
        tb = [bank[:, 4, :], bank[:, 5, :]]
        ob = bank[:, 6, 0:HH * (DH1 + 1)].rearrange("p (h d) -> p h d", h=HH)
        misc = bank[:, 7, :]

        w_in, folded = sem("weights_in"), sem("folded")
        kcur, vcur = sb("kcur", [P, DC, CL]), sb("vcur", [CL, H1, DH1 + 1])
        kv_ready = count("kv_ready", 1)
        kv_done, k_out, v_out = sem("kv_done"), sem("k_out"), sem("v_out")
        x_in, r_in = [sem(f"x_in{t}") for t in range(QT)], [sem(f"r_in{t}") for t in range(QT)]
        x2_out, x3_out = [sem(f"x2_out{t}") for t in range(QT)], [sem(f"x3_out{t}") for t in range(QT)]
        g_in = [[sem(f"g_in{s}{c}") for c in range(2)] for s in range(2)]
        icopied = count("icopied", QT)
        x_biased = count("x_biased", QT)
        summed, x2_ready = count("summed", QT), count("x2_ready", QT, 2)
        bn_step, stat, rst, veps_step = count("bn_step", QT), count("stat", QT), count("rst", QT), count("veps_step", QT)
        y_ready, y_read = count("y_ready", QT), count("y_read", QT, QT)
        xT_ready, q_done, qT_ready = count("xT_ready", QT), count("q_done", DC), count("qT_ready", DC)
        s_done, max_done = count("s_done", U1), count("max_done", U1)
        p_ready, exp_done = count("p_ready", U1, 2), count("exp_done", U1)
        t_done, pt_ready = count("t_done", 2 * U1, 2), count("pt_ready", 2 * U1, 2)
        pv_done, rinv_step, o_ready = count("pv_done", U1, 2), count("rinv_step", U1), count("o_ready", U1, 1)
        ot_done, ot_ready = count("ot_done", QT, 2), count("ot_ready", QT)
        wo_done, r_biased, x3_ready = count("wo_done", QT, 2), count("r_biased", QT), count("x3_ready", QT)
        bn3_step, stat3, rst3, veps3_step = count("bn3_step", QT), count("stat3", QT), count("rst3", QT), count("veps3_step", QT)
        n3_ready, n3_read, n3T_ready = count("n3_ready", QT, QT), count("n3_read", QT, 2), count("n3T_ready", QT)
        lg_done, lg_out = count("lg_done", QT, 2), count("lg_out", QT, QT)

        def rounds(eng, body):
            with eng.Fori(0, 3) as b:
                body(b, True)
            body(3, False)
            with eng.Fori(4, B - 1) as b:
                body(b, False)
            body(B - 1, None)

        def credit(eng, *counts):
            for c in counts:
                eng.sem_inc(c.sem, c.credit)

        with nc.Block() as block:
            @block.sync
            def _(sp):
                for dst, src in ((wq, "wq1"), (wk, "wk1"), (wv, "wv1"), (wo, "wo1"), (gw, "gw1"), (ctxT, "ctxT")):
                    sp.dma_start(dst[:, :, :], ins[src].rearrange("(c p) n -> p c n", p=P)).then_inc(w_in, 16)
                for dst, src in ((bq, "bq1"), (bk, "bk1")):
                    sp.dma_start(dst[:, :], ins[src]).then_inc(w_in, 16)
                for dst, src in ((bv, "bv1"), (bo, "bo1"), (bf, "bf0")):
                    sp.dma_start(dst[:, :], ins[src][None, :].to_broadcast([P, D])).then_inc(w_in, 16)

                def load_x(b, first):
                    for t in range(QT):
                        sp.wait_ge(x2_out[t], b * 16 + 16)
                        sp.nop(nofuse=True)
                        if not first:
                            sp.wait_ge(y_ready.sem, y_ready.have(b, t) - QT)
                            sp.nop(nofuse=True)
                        sp.dma_start(X[:, t, :], k.x1[ds(b * S + t * P, P), :]).then_inc(x_in[t], 16)

                def store_x2(b):
                    for t in range(QT):
                        sp.wait_ge(x2_ready.sem, x2_ready.have(b, t))
                        sp.dma_start(k.x2[ds(b * S + t * P, P), :], X[:, t, :]).then_inc(x2_out[t], 16)

                load_x(0, True)
                store_x2(0)

                def body(b, succ):
                    for t in range(QT):
                        sp.wait_ge(x2_out[t], b * 16 + 32)
                        sp.nop(nofuse=True)
                        sp.wait_ge(x3_out[t], b * 16 + 16)
                        sp.nop(nofuse=True)
                        sp.wait_ge(n3_ready.sem, n3_ready.back(b, t, QT))
                        sp.nop(nofuse=True)
                        sp.dma_start(R[:, t, :], k.x2[ds(b * S + t * P, P), :]).then_inc(r_in[t], 16)
                    if succ is not None:
                        load_x(b + 1, False)
                        store_x2(b + 1)
                    for t in range(QT):
                        sp.wait_ge(x3_ready.sem, x3_ready.have(b, t))
                        sp.dma_start(k.x3[ds(b * S + t * P, P), :], R[:, t, :]).then_inc(x3_out[t], 16)
                rounds(sp, body)
                for t in range(QT):
                    sp.wait_ge(x3_out[t], 16 * (B + 1))

            @block.gpsimd
            def _(pool):
                for t in range(QT):
                    pool.sem_inc(x2_out[t], 16)
                    pool.sem_inc(x3_out[t], 16)
                pool.wait_ge(w_in, 16 * 11)
                pool.tensor_scalar(bo[:, :], bo[:, :], k.gate[:, 1:2], None, ALU.mult).then_inc(folded, 1)
                pool.tensor_scalar(bf[:, :], bf[:, :], k.gate[:, 2:3], None, ALU.mult).then_inc(folded, 1)
                pool.memset(V[:, :, :, DH1:DH1 + 1], 1.0).then_inc(folded, 1)
                pool.wait_ge(folded, 3)

                def prep(b, comb):
                    def fetch(t):
                        s = t % 2
                        pool.wait_ge(x2_ready.sem, x2_ready.back(b, t, 2))
                        for c in range(2):
                            pool.tensor_copy(icol[:, s, c:c + 1], k.slot0[:, ds(b * QT + (c * NA0 // 2 + t), 1)])
                            i = pool.tensor_copy(wcol[:, s, c:c + 1], k.w0[:, ds(b * QT + (c * NA0 // 2 + t), 1)])
                        i.then_inc(icopied.sem, 1)
                        pool.wait_ge(icopied.sem, icopied.have(b, t))
                        pool.nop(nofuse=True)
                        for c in range(2):
                            pool.indirect_dma_start(G[:, s, c, :], None, k.y0, bass.IndirectOffsetOnAxis(icol[:, s, c:c + 1], 0))\
                                .then_inc(g_in[s][c], 16)

                    def finish(t):
                        pool.wait_ge(stat.sem, stat.have(b, t))
                        pool.nop(nofuse=True)
                        pool.tensor_scalar(veps[:, t:t + 1], mv[:, t, 1:2], EPS, None, ALU.add).then_inc(veps_step.sem, 1)
                        pool.wait_ge(veps_step.sem, veps_step.have(b, t))
                        pool.tensor_tensor(rstd[:, t:t + 1], veps[:, t:t + 1], k.halfneg[:, 0:1], ALU.pow).then_inc(rst.sem, 1)

                    for t in range(QT):
                        pool.wait_ge(x_in[t], b * 16 + 16)
                        pool.tensor_tensor(X[:, t, :], X[:, t, :], bf[:, :], ALU.add).then_inc(x_biased.sem, 1)
                    if comb:
                        fetch(0)
                        fetch(1)
                    for t in range(QT):
                        finish(t)
                        if comb and t + 2 < QT:
                            fetch(t + 2)

                pool.wait_ge(k_out, 2 * DC)
                pool.wait_ge(v_out, B)
                prep(0, True)

                def body(b, succ):
                    pool.wait_ge(pv_done.sem, pv_done.have(b, -1))
                    pool.tensor_copy(kcur[:, :, :], kT[:, :, ds(b * CL, CL)])
                    pool.tensor_copy(vcur[:, :, :], V[:, ds(b, 1), :, :].rearrange("p o h d -> p (o h) d")).then_inc(kv_ready.sem, 1)
                    for t in range(QT):
                        pool.wait_ge(r_in[t], b * 16 + 16)
                        pool.tensor_tensor(R[:, t, :], R[:, t, :], bo[:, :], ALU.add).then_inc(r_biased.sem, 1)
                    if succ is not None:
                        prep(b + 1, succ)
                    for t in range(QT):
                        pool.wait_ge(stat3.sem, stat3.have(b, t))
                        pool.nop(nofuse=True)
                        pool.tensor_scalar(veps3[:, t:t + 1], mv3[:, t, 1:2], EPS, None, ALU.add).then_inc(veps3_step.sem, 1)
                        pool.wait_ge(veps3_step.sem, veps3_step.have(b, t))
                        pool.tensor_tensor(rstd3[:, t:t + 1], veps3[:, t:t + 1], k.halfneg[:, 0:1], ALU.pow).then_inc(rst3.sem, 1)
                rounds(pool, body)

            @block.tensor
            def _(pe):
                credit(pe, y_read, t_done, pv_done, ot_done, wo_done, n3_read, lg_done)
                pe.wait_ge(w_in, 16 * 11)
                pe.wait_ge(folded, 3)
                for n in range(2 * DC):
                    m, half = n // 2, n % 2
                    if n >= 2:
                        pe.wait_ge(k_out, n - 1)
                    for c in range(CC):
                        mm = nc.tensor.matmul(bank[:, n % 2, 0:4 * CL], wk[:, c, m * P:m * P + P],
                                              ctxT[:, c, half * 4 * CL:(half + 1) * 4 * CL], start=(c == 0), stop=(c == CC - 1))
                    mm.then_inc(kv_done, 1)
                for b in range(B):
                    if b >= 2:
                        pe.wait_ge(v_out, b - 1)
                    for c in range(CC):
                        mm = nc.tensor.matmul(bank[0:CL, 2 + b % 2, :], ctxT[:, c, b * CL:b * CL + CL], wv[:, c, :],
                                              start=(c == 0), stop=(c == CC - 1))
                    mm.then_inc(kv_done, 1)
                pe.wait_ge(k_out, 2 * DC)
                pe.wait_ge(v_out, B)

                def body(b, succ):
                    for t in range(QT):
                        pe.wait_ge(y_ready.sem, y_ready.have(b, t))
                        for c in range(DC):
                            mm = nc.tensor.transpose(bank[:, t, c * P:c * P + P], Y[:, t, c * P:c * P + P], k.ident[:, :])
                        mm.then_inc(y_read.sem, 1)
                    pe.wait_ge(xT_ready.sem, xT_ready.have(b, QT - 1))
                    for m in range(DC):
                        for c in range(DC):
                            mm = nc.tensor.matmul(bank[:, m, :], wq[:, c, m * P:m * P + P], xT[:, c, :],
                                                  start=(c == 0), stop=(c == DC - 1))
                        mm.then_inc(q_done.sem, 1)
                    pe.wait_ge(qT_ready.sem, qT_ready.have(b, DC - 1))
                    pe.wait_ge(kv_ready.sem, kv_ready.have(b, 0))

                    def scores(u):
                        t, half = u // 2, u % 2
                        pe.wait_ge(p_ready.sem, p_ready.back(b, u, 2))
                        for i in range(HH):
                            c, r2 = i // 2, i % 2
                            r = DH1 * (2 * half + r2)
                            mm = nc.tensor.matmul(Sb[half][:, r2, c, :], qT[r:r + DH1, c, t * P:t * P + P],
                                                  kcur[r:r + DH1, c, :], start=True, stop=True)
                        mm.then_inc(s_done.sem, 1)

                    def turn(u):
                        pe.wait_ge(exp_done.sem, exp_done.have(b, u))
                        for q in range(2):
                            pe.wait_ge(pt_ready.sem, pt_ready.back(b, 2 * u + q, 2))
                            for i in range(4):
                                mm = nc.tensor.transpose(tb[q][0:CL, i * P:i * P + P], Pr[:, u % 2, 4 * q + i, :], k.ident[:, :])
                            mm.then_inc(t_done.sem, 1)

                    def pv(u):
                        half = u % 2
                        pe.wait_ge(pt_ready.sem, pt_ready.have(b, 2 * u + 1))
                        pe.wait_ge(o_ready.sem, o_ready.back(b, u, 1))
                        for i in range(HH):
                            mm = nc.tensor.matmul(ob[:, i, :], PT[:, u % 2, 4 * (i % 2) + i // 2, :],
                                                  vcur[:, 4 * (i // 2) + 2 * half + i % 2, :], start=True, stop=True)
                        mm.then_inc(pv_done.sem, 1)

                    last = [lambda: pe.wait_ge(lg_out.sem, lg_out.back(b, QT - 1, QT))]

                    def o_turn(t):
                        last[0]()
                        pe.wait_ge(o_ready.sem, o_ready.have(b, 2 * t + 1))
                        for c in range(DC):
                            mm = nc.tensor.transpose(misc[:, c * P:c * P + P], O[:, t % 2, c * P:c * P + P], k.ident[:, :])
                        mm.then_inc(ot_done.sem, 1)
                        last[0] = lambda: pe.wait_ge(ot_ready.sem, ot_ready.have(b, t))

                    def out(t):
                        last[0]()
                        pe.wait_ge(ot_ready.sem, ot_ready.have(b, t))
                        for c in range(DC):
                            mm = nc.tensor.matmul(misc, OT[:, t % 2, c, :], wo[:, c, :], start=(c == 0), stop=(c == DC - 1))
                        mm.then_inc(wo_done.sem, 1)
                        last[0] = lambda: pe.wait_ge(x3_ready.sem, x3_ready.have(b, t))

                    def n_turn(t):
                        last[0]()
                        pe.wait_ge(n3_ready.sem, n3_ready.have(b, t))
                        for c in range(DC):
                            mm = nc.tensor.transpose(misc[:, c * P:c * P + P], N3[:, t % 2, c * P:c * P + P], k.ident[:, :])
                        mm.then_inc(n3_read.sem, 1)
                        last[0] = lambda: pe.wait_ge(n3T_ready.sem, n3T_ready.have(b, t))

                    def router(t):
                        last[0]()
                        pe.wait_ge(n3T_ready.sem, n3T_ready.have(b, t))
                        for c in range(DC):
                            mm = nc.tensor.matmul(misc[:, 0:E], N3T[:, t % 2, c, :], gw[:, c, :], start=(c == 0), stop=(c == DC - 1))
                        mm.then_inc(lg_done.sem, 1)
                        last[0] = lambda: pe.wait_ge(lg_out.sem, lg_out.have(b, t))

                    for u in range(2 * QT + 8):
                        if u < U1:
                            scores(u)
                        if 1 <= u <= U1:
                            turn(u - 1)
                        if 2 <= u <= U1 + 1:
                            pv(u - 2)
                        for f, lag in ((o_turn, 4), (out, 5), (n_turn, 8), (router, 9)):
                            if u >= lag and (u - lag) % 2 == 0 and (u - lag) // 2 < QT:
                                f((u - lag) // 2)

                rounds(pe, body)

            @block.scalar
            def _(act):
                credit(act, pt_ready)
                act.wait_ge(folded, 3)
                for n in range(2 * DC):
                    m, half = n // 2, n % 2
                    act.wait_ge(kv_done, n + 1)
                    act.activation(kT[:, m, half * 4 * CL:(half + 1) * 4 * CL], bank[:, n % 2, 0:4 * CL], ACT.Identity,
                                   bias=bk[:, m:m + 1]).then_inc(k_out, 1)

                def body(b, succ):
                    for t in range(QT):
                        act.wait_ge(y_read.sem, y_read.have(b, t))
                        act.activation(xT[:, :, t * P:t * P + P], bank[:, t, :].rearrange("p (c n) -> p c n", c=DC), ACT.Copy)\
                            .then_inc(xT_ready.sem, 1)
                    for m in range(DC):
                        act.wait_ge(q_done.sem, q_done.have(b, m))
                        act.activation(qT[:, m, :], bank[:, m, :], ACT.Identity, bias=bq[:, m:m + 1]).then_inc(qT_ready.sem, 1)
                    for u in range(2 * QT + 8):
                        if u < U1:
                            act.wait_ge(p_ready.sem, p_ready.have(b, u))
                            act.activation(Pr[:, u % 2, :, :], Pr[:, u % 2, :, :], ACT.Exp, scale=DH1 ** -0.5)\
                                .then_inc(exp_done.sem, 1)
                        if 1 <= u <= U1:
                            for q in range(2):
                                act.wait_ge(t_done.sem, t_done.have(b, 2 * (u - 1) + q))
                                if q == 0:
                                    act.wait_ge(pv_done.sem, pv_done.back(b, u - 1, 2))
                                act.activation(PT[:, (u - 1) % 2, 4 * q:4 * q + 4, :],
                                               tb[q][0:CL, :].rearrange("p (h n) -> p h n", h=4), ACT.Copy)\
                                    .then_inc(pt_ready.sem, 1)
                        if u >= 4 and (u - 4) % 2 == 0 and (u - 4) // 2 < QT:
                            t = (u - 4) // 2
                            act.wait_ge(ot_done.sem, ot_done.have(b, t))
                            act.wait_ge(wo_done.sem, wo_done.back(b, t, 2))
                            act.activation(OT[:, t % 2, :, :], misc.rearrange("p (c n) -> p c n", c=DC), ACT.Copy)\
                                .then_inc(ot_ready.sem, 1)
                        if u >= 8 and (u - 8) % 2 == 0 and (u - 8) // 2 < QT:
                            t = (u - 8) // 2
                            act.wait_ge(n3_read.sem, n3_read.have(b, t))
                            act.wait_ge(lg_done.sem, lg_done.back(b, t, 2))
                            act.activation(N3T[:, t % 2, :, :], misc.rearrange("p (c n) -> p c n", c=DC), ACT.Copy)\
                                .then_inc(n3T_ready.sem, 1)
                rounds(act, body)

            @block.vector
            def _(dve):
                credit(dve, x2_ready, p_ready, o_ready, lg_out, n3_ready)
                dve.wait_ge(folded, 3)
                for b in range(B):
                    dve.wait_ge(kv_done, 2 * DC + b + 1)
                    dve.tensor_tensor(V[:, b, :, 0:DH1], bank[0:CL, 2 + b % 2, :].rearrange("p (h d) -> p h d", h=H1),
                                      bv[0:CL, :].rearrange("p (h d) -> p h d", h=H1), ALU.add).then_inc(v_out, 1)

                def prep_a(b, t, comb):
                    s = t % 2
                    dve.wait_ge(x_biased.sem, x_biased.have(b, t))
                    if comb:
                        for c in range(2):
                            dve.wait_ge(g_in[s][c], b * 32 + 16 * (t // 2 + 1))
                        dve.scalar_tensor_tensor(X[:, t, :], G[:, s, 0, :], wcol[:, s, 0:1], X[:, t, :], ALU.mult, ALU.add)\
                            .then_inc(summed.sem, 1)
                        dve.wait_ge(summed.sem, summed.have(b, t))
                        dve.scalar_tensor_tensor(X[:, t, :], G[:, s, 1, :], wcol[:, s, 1:2], X[:, t, :], ALU.mult, ALU.add)\
                            .then_inc(x2_ready.sem, 1)
                        dve.wait_ge(x2_ready.sem, x2_ready.have(b, t))
                    else:
                        dve.sem_inc(x2_ready.sem, 1)
                    dve.bn_stats(bst[:, t, :], X[:, t, :]).then_inc(bn_step.sem, 1)
                    dve.wait_ge(bn_step.sem, bn_step.have(b, t))
                    dve.nop(nofuse=True)
                    dve.bn_aggr(mv[:, t, :], bst[:, t, :]).then_inc(stat.sem, 1)

                def prep_b(b, t):
                    dve.wait_ge(rst.sem, rst.have(b, t))
                    dve.wait_ge(y_read.sem, y_read.back(b, t, QT))
                    dve.tensor_scalar(Y[:, t, :], X[:, t, :], mv[:, t, 0:1], rstd[:, t:t + 1], ALU.subtract, ALU.mult)\
                        .then_inc(y_ready.sem, 1)

                for t in range(QT):
                    prep_a(0, t, True)
                    prep_b(0, t)

                def body(b, succ):
                    for u in range(2 * QT + 8):
                        if u < U1:
                            s = u % 2
                            dve.wait_ge(s_done.sem, s_done.have(b, u))
                            dve.tensor_reduce(smax[:, s, :].rearrange("p (r c) -> p r c", r=2), Sb[s], AX.X, ALU.max)\
                                .then_inc(max_done.sem, 1)
                            dve.wait_ge(max_done.sem, max_done.have(b, u))
                            dve.wait_ge(t_done.sem, t_done.back(b, 2 * u + 1, 2) - 2)
                            dve.tensor_tensor(Pr[:, s, :, :].rearrange("p (r c) n -> p r c n", r=2), Sb[s],
                                              smax[:, s, :].rearrange("p (r c) -> p r c", r=2).unsqueeze(3)
                                              .to_broadcast([P, 2, 4, CL]), ALU.subtract).then_inc(p_ready.sem, 1)
                        if 2 <= u <= U1 + 1:
                            v = u - 2
                            dve.wait_ge(pv_done.sem, pv_done.have(b, v))
                            dve.wait_ge(ot_done.sem, ot_done.back(b, v // 2, 2))
                            dve.reciprocal(rinv[:, v % 2, :], ob[:, :, DH1]).then_inc(rinv_step.sem, 1)
                            dve.wait_ge(rinv_step.sem, rinv_step.have(b, v))
                            half = v % 2
                            dve.tensor_tensor(O[:, (v // 2) % 2, :].rearrange("p (c r d) -> p c r d", c=4, r=4)
                                              [:, :, 2 * half:2 * half + 2, :],
                                              ob[:, :, 0:DH1].rearrange("p (c r) d -> p c r d", r=2),
                                              rinv[:, half, :].rearrange("p (c r) -> p c r", r=2).unsqueeze(3)
                                              .to_broadcast([P, 4, 2, DH1]), ALU.mult).then_inc(o_ready.sem, 1)
                        if u >= 5 and (u - 5) % 2 == 0 and (u - 5) // 2 < QT:
                            t = (u - 5) // 2
                            dve.wait_ge(wo_done.sem, wo_done.have(b, t))
                            dve.wait_ge(r_biased.sem, r_biased.have(b, t))
                            dve.scalar_tensor_tensor(R[:, t, :], misc, k.gate[:, 1:2], R[:, t, :], ALU.mult, ALU.add)\
                                .then_inc(x3_ready.sem, 1)
                            dve.wait_ge(x3_ready.sem, x3_ready.have(b, t))
                            dve.bn_stats(bst3[:, t, :], R[:, t, :]).then_inc(bn3_step.sem, 1)
                            dve.wait_ge(bn3_step.sem, bn3_step.have(b, t))
                            dve.nop(nofuse=True)
                            dve.bn_aggr(mv3[:, t, :], bst3[:, t, :]).then_inc(stat3.sem, 1)
                        if u >= 7 and (u - 7) % 2 == 0 and (u - 7) // 2 < QT:
                            t = (u - 7) // 2
                            dve.wait_ge(rst3.sem, rst3.have(b, t))
                            dve.wait_ge(n3_read.sem, n3_read.back(b, t, 2))
                            dve.tensor_scalar(N3[:, t % 2, :], R[:, t, :], mv3[:, t, 0:1], rstd3[:, t:t + 1],
                                              ALU.subtract, ALU.mult).then_inc(n3_ready.sem, 1)
                        if u >= 9 and (u - 9) % 2 == 0 and (u - 9) // 2 < QT:
                            t = (u - 9) // 2
                            dve.wait_ge(lg_done.sem, lg_done.have(b, t))
                            dve.tensor_copy(k.logits[:, ds(b * QT + t, 1), :].rearrange("p o e -> p (o e)"), misc[:, 0:E])\
                                .then_inc(lg_out.sem, 1)
                        if succ is not None and u < U1:
                            (prep_a(b + 1, u // 2, succ) if u % 2 == 0 else prep_b(b + 1, u // 2))
                rounds(dve, body)


def combine(nc, k, out):
    RING = 4
    NT = B * QT
    with ExitStack() as ctx:
        sb = lambda n, s, d=F32: ctx.enter_context(nc.sbuf_tensor("c_" + n, s, d))
        sem = lambda n: k.sems.enter_context(nc.semaphore("c_" + n))
        count = lambda n, per, credit=0: Count(k.sems, nc, "c_" + n, per, credit)
        X, G = sb("X", [P, RING, D]), sb("G", [P, RING, 2, D])
        icol, wcol = sb("icol", [P, RING, 2], I32), sb("wcol", [P, RING, 2])
        x_in, x_out = [sem(f"x_in{q}") for q in range(RING)], [sem(f"x_out{q}") for q in range(RING)]
        g_in = [[sem(f"g_in{q}{c}") for c in range(2)] for q in range(RING)]
        icopied, half, done = count("icopied", RING), count("half", RING), count("done", RING, RING)
        with nc.Block() as block:
            @block.sync
            def _(sp):
                with sp.Fori(0, NT // RING) as i:
                    for q in range(RING):
                        sp.wait_ge(x_out[q], i * 16 + 16)
                        sp.dma_start(X[:, q, :], k.x3[ds((i * RING + q) * P, P), :]).then_inc(x_in[q], 16)

            @block.gpsimd
            def _(pool):
                with pool.Fori(0, NT // RING) as i:
                    for q in range(RING):
                        pool.wait_ge(done.sem, done.back(i, q, RING))
                        for c in range(2):
                            pool.tensor_copy(icol[:, q, c:c + 1], k.slot1[:, ds(i * RING + (q + c * NT), 1)])
                            last = pool.tensor_copy(wcol[:, q, c:c + 1], k.w1[:, ds(i * RING + (q + c * NT), 1)])
                        last.then_inc(icopied.sem, 1)
                        pool.wait_ge(icopied.sem, icopied.have(i, q))
                        pool.nop(nofuse=True)
                        for c in range(2):
                            pool.indirect_dma_start(G[:, q, c, :], None, k.y1, bass.IndirectOffsetOnAxis(icol[:, q, c:c + 1], 0))\
                                .then_inc(g_in[q][c], 16)

            @block.vector
            def _(dve):
                dve.sem_inc(done.sem, done.credit)
                with dve.Fori(0, NT // RING) as i:
                    for q in range(RING):
                        dve.wait_ge(x_in[q], i * 16 + 16)
                        dve.wait_ge(g_in[q][0], i * 16 + 16)
                        dve.scalar_tensor_tensor(X[:, q, :], G[:, q, 0, :], wcol[:, q, 0:1], X[:, q, :], ALU.mult, ALU.add)\
                            .then_inc(half.sem, 1)
                        dve.wait_ge(half.sem, half.have(i, q))
                        dve.wait_ge(g_in[q][1], i * 16 + 16)
                        dve.scalar_tensor_tensor(X[:, q, :], G[:, q, 1, :], wcol[:, q, 1:2], X[:, q, :], ALU.mult, ALU.add)\
                            .then_inc(done.sem, 1)

            @block.scalar
            def _(act):
                for q in range(RING):
                    act.sem_inc(x_out[q], 16)
                with act.Fori(0, NT // RING) as i:
                    for q in range(RING):
                        act.wait_ge(done.sem, done.have(i, q))
                        act.dma_start(out[ds((i * RING + q) * P, P), :], X[:, q, :]).then_inc(x_out[q], 16)
                for q in range(RING):
                    act.wait_ge(x_out[q], 16 * (NT // RING + 1))


INS = ["x", "ctx", "mask", "g_xattn", "g_ffn", "wqT", "wlkvT", "wkvT", "woT", "lng", "lnb", "lxg", "lxb",
       "qng", "kng", "bo0", "ei", "ew", "w1_0", "w2_0", "bf0", "wq1", "wk1", "wv1", "wo1", "bq1", "bk1", "bv1", "bo1",
       "gw1", "ctxT", "w1_1", "w2_1", "w3_1"]


def build(nc, ins, out):
    k = Core()
    with ExitStack() as ctx:
        k.sems = ctx
        sb = lambda n, s, d=F32: ctx.enter_context(nc.sbuf_tensor(n, s, d))
        k.ident, k.tri, k.ones = sb("ident", [P, P]), sb("tri", [P, P]), sb("ones", [P, P])
        k.halfneg, k.gate = sb("halfneg", [P, 16]), sb("gate", [P, 4])
        k.iota_e, k.iota_p, k.tokcol = sb("iota_e", [P, E]), sb("iota_p", [P, P]), sb("tokcol", [P, B * QT])
        k.bank = ctx.enter_context(nc.psum_tensor("bank", [P, 8, 512], F32))
        k.slot0, k.slot1 = sb("slot0", [P, NA0], I32), sb("slot1", [P, NA1], I32)
        k.idx0, k.idx1 = sb("idx0", [P, NT0 * ROWS // P], I32), sb("idx1", [P, NT1 * ROWS // P], I32)
        k.te0, k.te1 = sb("te0", [1, NT0], I32), sb("te1", [1, NT1], I32)
        k.w0, k.w1 = sb("w0", [P, NA0]), sb("w1", [P, NA1])
        k.logits = sb("logits", [P, B * QT, E])
        dram = lambda n, rows: nc.dram_tensor(n, [rows, D], F32, kind="Internal").ap()
        k.x1, k.x2, k.x3 = dram("x1", NTOK), dram("x2", NTOK), dram("x3", NTOK)
        k.y0, k.y1 = dram("y0", NT0 * ROWS), dram("y1", NT1 * ROWS)
        setup(nc, k, ins)
        attention0(nc, k, ins)
        route_given(nc, k, ins)
        experts(nc, k, "e0_", k.x1, ins["w1_0"], None, ins["w2_0"], FF0, NT0, k.idx0, k.te0, k.y0)
        attention1(nc, k, ins)
        route_top2(nc, k)
        experts(nc, k, "e1_", k.x3, ins["w1_1"], ins["w3_1"], ins["w2_1"], FF1, NT1, k.idx1, k.te1, k.y1)
        combine(nc, k, out)


def kernel(**inputs):
    import numpy as np
    import concourse.bacc as bacc
    from concourse.bass_utils import run_bass_kernel_spmd

    columns = lambda v: v.reshape(-1, P).T
    assigned = lambda v: v.reshape(-1, P, 2).transpose(1, 2, 0).reshape(P, -1)
    a = {n: np.asarray(v) for n, v in inputs.items()}
    host = {
        "x": a["x"].reshape(NTOK, D), "ctx": a["ctx_768"].reshape(B * CL, CD),
        "mask": a["mask_BxS2_bk0"], "g_xattn": a["g_xattn"], "g_ffn": a["g_ffn"],
        "wqT": a["L0_xattn_Wq"].T, "wlkvT": a["L0_xattn_Wlkv"].T, "wkvT": a["L0_xattn_Wkv"].T,
        "woT": a["L0_xattn_Wo"].T, "lng": columns(a["L0_xattn_ln_l_g"]), "lnb": columns(a["L0_xattn_ln_l_b"]),
        "lxg": columns(a["L0_xattn_ln_x_g"]), "lxb": columns(a["L0_xattn_ln_x_b"]), "qng": a["L0_xattn_qn_g"],
        "kng": a["L0_xattn_kn_g"], "bo0": a["L0_xattn_bo"],
        "ei": assigned(a["L0_ffn_expert_indices"]), "ew": assigned(a["L0_ffn_expert_weights"]),
        "w1_0": a["L0_ffn_w1"], "w2_0": a["L0_ffn_w2"], "bf0": a["L0_ffn_bias"],
        "wq1": a["L1_xattn_wq"], "wk1": a["L1_xattn_wk"], "wv1": a["L1_xattn_wv"], "wo1": a["L1_xattn_wo"],
        "bq1": columns(a["L1_xattn_bq"]), "bk1": columns(a["L1_xattn_bk"]), "bv1": a["L1_xattn_bv"],
        "bo1": a["L1_xattn_bo"], "gw1": a["L1_ffn_gate_w"].T, "ctxT": a["ctx_768"].reshape(B * CL, CD).T,
        "w1_1": a["L1_ffn_w1"], "w2_1": a["L1_ffn_w2"], "w3_1": a["L1_ffn_w3"],
    }
    nc = bacc.Bacc("TRN2", target_bir_lowering=False, num_devices=1)
    arrays, ins = {}, {}
    for name in INS:
        v = np.ascontiguousarray(host[name])
        arrays["in_" + name] = v
        ins[name] = nc.dram_tensor("in_" + name, v.shape, mybir.dt.from_np(v.dtype), kind="ExternalInput").ap()
    out = nc.dram_tensor("out_0", (NTOK, D), F32, kind="ExternalOutput").ap()
    build(nc, ins, out)
    r = run_bass_kernel_spmd(nc, [arrays], core_ids=[0])
    return r.results[0]["out_0"].reshape(B, S, D)
```

```python
from contextlib import ExitStack

import concourse.bass as bass
from concourse import mybir

F32 = mybir.dt.float32
F32R = mybir.dt.float32r
I32 = mybir.dt.int32
U8 = mybir.dt.uint8
ALU = mybir.AluOpType
ACT = mybir.ActivationFunctionType
AX = mybir.AxisListType

P = 128
D = 512
DC = D // P
B, S = 8, 512
QT = S // P
NTOK = B * S
CL, CD = 120, 384
CC = CD // P
KEYS = S + CL
EPS = 1e-5
E = 8
ROWS = 256
TOK0 = 2048
NA0 = 2 * TOK0 // P
NA1 = 2 * NTOK // P
NT0 = 2 * TOK0 // ROWS + E - 1
NT1 = 2 * NTOK // ROWS + E - 1
FF0, FF1 = 2048, 1024
MASKED = -1e30


class Count:

    def __init__(self, ctx, nc, name, per, credit=0):
        self.sem = ctx.enter_context(nc.semaphore(name))
        self.per, self.credit = per, credit

    def have(self, b, j):
        return b * self.per + (j + 1 + self.credit)

    def back(self, b, j, depth):
        assert self.credit >= depth
        return b * self.per + (j + 1 + self.credit - depth)


def ds(a, n):
    return bass.ds(a, n)


class Semaphores:

    def __init__(self, nc):
        self.nc, self.all = nc, []

    def enter_context(self, made):
        self.all.append(made.__enter__())
        return self.all[-1]

    def give_back(self):
        self.nc.clear_and_free_semaphores(self.all)
        self.nc.all_engine_barrier()


class Core:
    pass


def setup(nc, k, ins):
    with ExitStack() as ctx:
        sem = lambda n: k.sems.enter_context(nc.semaphore(n))
        zeroed, masks, loaded, tanhed = sem("zeroed"), sem("masks"), sem("setup_loaded"), sem("tanhed")
        graw = ctx.enter_context(nc.sbuf_tensor("graw", [P, 4], F32))
        with nc.Block() as block:
            @block.gpsimd
            def _(pool):
                pool.memset(k.ident[:, :], 0.0).then_inc(zeroed, 1)
                pool.memset(k.tri[:, :], 1.0).then_inc(zeroed, 1)
                pool.memset(k.ones[:, :], 1.0)
                pool.memset(k.halfneg[:, :], -0.5)
                pool.iota(k.iota_e[:, :], [[1, E]], base=0, channel_multiplier=0,
                          allow_small_or_imprecise_dtypes=True)
                pool.iota(k.iota_p[:, :], [[1, P]], base=0, channel_multiplier=0,
                          allow_small_or_imprecise_dtypes=True)
                pool.iota(k.tokcol[:, :], [[P, B * QT]], base=0, channel_multiplier=1,
                          allow_small_or_imprecise_dtypes=True)
                pool.wait_ge(zeroed, 2)
                pool.affine_select(out=k.ident[:, :], in_=k.ident[:, :], compare_op=ALU.not_equal, fill=1.0,
                                   base=0, pattern=[[-1, P]], channel_multiplier=1).then_inc(masks, 1)
                pool.affine_select(out=k.tri[:, :], in_=k.tri[:, :], compare_op=ALU.is_gt, fill=0.0,
                                   base=0, pattern=[[1, P]], channel_multiplier=-1).then_inc(masks, 1)
                pool.wait_ge(masks, 2)

            @block.sync
            def _(sp):
                sp.dma_start(graw[:, 0:2], ins["g_xattn"][None, :].to_broadcast([P, 2])).then_inc(loaded, 16)
                sp.dma_start(graw[:, 2:4], ins["g_ffn"][None, :].to_broadcast([P, 2])).then_inc(loaded, 16)

            @block.scalar
            def _(act):
                act.wait_ge(loaded, 32)
                act.activation(k.gate[:, :], graw[:, :], ACT.Tanh).then_inc(tanhed, 1)
                act.wait_ge(tanhed, 1)


LN_PIECES = [("a", 0), ("a", 1), ("b", 0), ("a", 2), ("b", 1), ("c", 0), ("a", 3), ("b", 2), ("c", 1),
             ("a", 4), ("b", 3), ("c", 2), ("c", 3), ("b", 4)]
LN_STATS = [q for q in LN_PIECES if q[0] == "a" or (q[0] == "b" and q[1] < 4)]
H0 = 8
DH0 = D // H0
U0 = H0 * QT
PRING = 4


def attention0(nc, k, ins):
    sems = Semaphores(nc)
    with ExitStack() as ctx:
        sb = lambda n, s, d=F32: ctx.enter_context(nc.sbuf_tensor("a0_" + n, s, d))
        sem = lambda n: sems.enter_context(nc.semaphore("a0_" + n))
        count = lambda n, per, credit=0: Count(sems, nc, "a0_" + n, per, credit)
        wq, wlkv, wkv, wo = sb("wq", [P, DC, D]), sb("wlkv", [P, DC, 2 * D]), sb("wkv", [P, CC, 2 * D]), sb("wo", [P, DC, D])
        lng, lnb, lxg, lxb = sb("lng", [P, DC]), sb("lnb", [P, DC]), sb("lxg", [P, CC]), sb("lxb", [P, CC])
        qg, kg, qgain = sb("qg", [P, 1]), sb("kg", [P, 1]), sb("qgain", [P, 1])
        bog = sb("bog", [P, D])
        mraw, mrow = sb("mraw", [1, B, CL], U8), sb("mrow", [1, B, CL], F32R)
        X, XC = sb("X", [P, QT, D]), sb("XC", [P, CD])
        Y, YC = sb("Y", [P, QT, D]), sb("YC", [P, CD])
        bst, mv = sb("bst", [P, 9, 6]), sb("mv", [P, 9, 2])
        veps, rstd = sb("veps", [P, 9]), sb("rstd", [P, 9])
        xT = sb("xT", [P, 2, DC, P])
        sq, ss, sc, rn = sb("sq", [P, 2 * D]), sb("ss", [P, 2 * H0]), sb("sc", [P, 2 * H0]), sb("rn", [P, 2 * H0])
        qkn = sb("qkn", [P, 2, 2 * D])
        Q2, KH, KL = sb("Q2", [P, H0, S], F32R), sb("KH", [P, H0, KEYS], F32R), sb("KL", [P, H0, KEYS], F32R)
        V = sb("V", [P, QT + 1, D])
        one_row = sb("one_row", [1, P], F32R)
        Pr, PT = sb("Pr", [P, PRING, KEYS]), sb("PT", [P, 2, QT + 1, S])
        nmax, rsum, rinv = sb("nmax", [P, 4]), sb("rsum", [P, 4]), sb("rinv", [P, 4])
        OT, R = sb("OT", [P, DC, S]), sb("R", [P, QT, D])
        bank = k.bank
        trb = bank[:, 0, :]
        qkbs, vb = [bank[:, 1:3, :], bank[:, 3:5, :]], bank[:, 5, :]
        tqb, tkb = bank[:, 6, :], bank[:, 7, :]
        Sb = [bank[:, 0:2, :].rearrange("p a b -> p (a b)"), bank[:, 2:4, :].rearrange("p a b -> p (a b)")]
        chunks = lambda bk: bk.rearrange("p (c n) -> p c n", c=DC)
        ptm, ptc, otb = [bank[:, 4, :], bank[:, 5, :]], bank[:, 6, :], bank[:, 7, :]

        w_in, folded, folding = sem("weights_in"), sem("folded"), sem("folding")
        n_w_in = 16 * 14
        x_in = [sem(f"x_in{t}") for t in range(QT + 1)]
        r_in = [sem(f"r_in{t}") for t in range(QT)]
        r_stored = [sem(f"r_stored{t}") for t in range(QT)]
        x_free = count("x_free", 5)
        ln_step = count("ln_step", 13)
        stat, rst = count("stat", 9), count("rstd_ready", 9)
        veps_step = count("veps_step", 9)
        y_ready, y_read = count("y_ready", 5), count("y_read", 5, 5)
        xT_ready = count("xT_ready", 5, 2)
        v_done, qk_done = count("v_done", 5), count("qk_done", 5, 2)
        squared, ss_done = count("squared", 5), count("ss_done", 5, 1)
        sc_step, rn_done = count("sc_step", 5), count("rn_done", 5, 1)
        qkn_ready, v_copied = count("qkn_ready", 5, 2), count("v_copied", 5, 1)
        tqk_done = count("tqk_done", 5, 2)
        high_ready, low_ready = count("high_ready", 5), count("low_ready", 5, 1)
        s_done, max_done, exp_done = count("s_done", U0), count("max_done", U0), count("exp_done", U0, 2)
        rinv_step, p_ready, t_done = count("rinv_step", U0), count("p_ready", U0), count("t_done", U0, PRING)
        ptm_out, ptc_out = count("ptm_out", U0, 2), count("ptc_out", H0, 1)
        pv_done, ot_out = count("pv_done", H0 // 2, 1), count("ot_out", H0 // 2, 1)
        wo_done, r_biased, x1_ready = count("wo_done", QT), count("r_biased", QT), count("x1_ready", QT, QT)

        def rounds(eng, body):
            with eng.Fori(0, B - 1) as b:
                body(b, True)
            body(B - 1, False)

        def credit(eng, *counts):
            for c in counts:
                eng.sem_inc(c.sem, c.credit)

        with nc.Block() as block:
            @block.sync
            def _(sp):
                def load_x(b):
                    for t in range(QT):
                        sp.dma_start(X[:, t, :], ins["x"][ds(b * S + t * P, P), :]).then_inc(x_in[t], 16)
                    sp.dma_start(XC[0:CL, :], ins["ctx"][ds(b * CL, CL), :]).then_inc(x_in[QT], 16)

                load_x(0)
                for dst, src in ((wq, "wqT"), (wlkv, "wlkvT"), (wkv, "wkvT"), (wo, "woT")):
                    sp.dma_start(dst[:, :, :], ins[src].rearrange("(c p) n -> p c n", p=P)).then_inc(w_in, 16)
                for dst, src in ((lng, "lng"), (lnb, "lnb"), (lxg, "lxg"), (lxb, "lxb")):
                    sp.dma_start(dst[:, :], ins[src]).then_inc(w_in, 16)
                for dst, src in ((qg, "qng"), (kg, "kng")):
                    for r in range(2):
                        sp.dma_start(dst[64 * r:64 * r + 64, :], ins[src][:, None]).then_inc(w_in, 16)
                sp.dma_start(bog[:, :], ins["bo0"][None, :].to_broadcast([P, D])).then_inc(w_in, 16)
                sp.dma_start(mraw[:, :, :], ins["mask"][None, :, :]).then_inc(w_in, 16)

                def body(b, more):
                    if more:
                        sp.wait_ge(x_free.sem, x_free.have(b, QT))
                        load_x(b + 1)
                    for t in range(QT):
                        sp.wait_ge(r_stored[t], b * 16 + 16)
                        sp.dma_start(R[:, t, :], ins["x"][ds(b * S + t * P, P), :]).then_inc(r_in[t], 16)
                    for t in range(QT):
                        sp.wait_ge(x1_ready.sem, x1_ready.have(b, t))
                        sp.dma_start(k.x1[ds(b * S + t * P, P), :], R[:, t, :]).then_inc(r_stored[t], 16)

                rounds(sp, body)
                for t in range(QT):
                    sp.wait_ge(r_stored[t], 16 * (B + 1))

            @block.gpsimd
            def _(pool):
                for t in range(QT):
                    pool.sem_inc(r_stored[t], 16)
                credit(pool, rn_done)

                def rstds(b):
                    for n, (kind, t) in enumerate(LN_STATS):
                        rows = CL if t == QT else P
                        pool.wait_ge(stat.sem, stat.have(b, n))
                        pool.nop(nofuse=True)
                        pool.tensor_scalar(veps[0:rows, n:n + 1], mv[0:rows, n, 1:2], EPS, None, ALU.add)\
                            .then_inc(veps_step.sem, 1)
                        pool.wait_ge(veps_step.sem, veps_step.have(b, n))
                        pool.tensor_tensor(rstd[0:rows, n:n + 1], veps[0:rows, n:n + 1], k.halfneg[0:rows, 0:1],
                                           ALU.pow).then_inc(rst.sem, 1)

                rstds(0)
                pool.wait_ge(w_in, n_w_in)
                pool.tensor_scalar(bog[:, :], bog[:, :], k.gate[:, 0:1], None, ALU.mult).then_inc(folded, 1)
                pool.tensor_tensor(qgain[:, :], qg[:, :], kg[:, :], ALU.mult).then_inc(folding, 1)
                pool.tensor_copy(one_row[:, :], k.ones[0:1, :]).then_inc(folding, 1)
                pool.wait_ge(folding, 2)
                pool.tensor_scalar(qgain[:, :], qgain[:, :], DH0 ** -0.5, None, ALU.mult).then_inc(folded, 1)
                pool.tensor_scalar(mrow[:, :, :], mraw[:, :, :], 1.0, -MASKED, ALU.subtract, ALU.mult).then_inc(folded, 1)
                pool.wait_ge(folded, 3)

                def body(b, more):
                    for t in range(QT + 1):
                        rows, c0 = (CL, H0) if t == QT else (P, 0)
                        pool.wait_ge(ss_done.sem, ss_done.have(b, t))
                        pool.nop(nofuse=True)
                        pool.tensor_scalar(sc[0:rows, c0:], ss[0:rows, c0:], 1.0 / DH0, 1e-16, ALU.mult, ALU.max)\
                            .then_inc(sc_step.sem, 1)
                        pool.wait_ge(sc_step.sem, sc_step.have(b, t))
                        pool.wait_ge(qkn_ready.sem, qkn_ready.back(b, t, 1))
                        pool.tensor_tensor(rn[0:rows, c0:], sc[0:rows, c0:], k.halfneg[0:rows, c0:],
                                           ALU.pow).then_inc(rn_done.sem, 1)
                    for t in range(QT):
                        pool.wait_ge(r_in[t], b * 16 + 16)
                        pool.tensor_tensor(R[:, t, :], R[:, t, :], bog[:, :], ALU.add).then_inc(r_biased.sem, 1)
                    if more:
                        rstds(b + 1)

                rounds(pool, body)

            @block.tensor
            def _(pe):
                credit(pe, y_read, qk_done, tqk_done, t_done, pv_done)
                pe.wait_ge(folded, 3)

                def body(b, more):
                    def tr(t):
                        rows, ch, src = (CL, CC, YC[0:CL, :]) if t == QT else (P, DC, Y[:, t, :])
                        pe.wait_ge(y_ready.sem, y_ready.have(b, t))
                        pe.wait_ge(xT_ready.sem, xT_ready.back(b, t, 1))
                        for c in range(ch):
                            mm = nc.tensor.transpose(trb[:, c * P:c * P + rows], src[:, c * P:c * P + P],
                                                     k.ident[0:rows, 0:rows])
                        mm.then_inc(y_read.sem, 1)

                    def proj(t):
                        rows, ch, kv = (CL, CC, wkv) if t == QT else (P, DC, wlkv)
                        pe.wait_ge(xT_ready.sem, xT_ready.have(b, t))
                        pe.wait_ge(v_copied.sem, v_copied.back(b, t, 1))
                        for c in range(ch):
                            mm = nc.tensor.matmul(vb[0:rows, :], xT[:, t % 2, c, 0:rows], kv[:, c, D:2 * D],
                                                  start=(c == 0), stop=(c == ch - 1))
                        mm.then_inc(v_done.sem, 1)
                        pe.wait_ge(qkn_ready.sem, qkn_ready.back(b, t, 2))
                        qkb = qkbs[t % 2]
                        if t < QT:
                            for c in range(ch):
                                nc.tensor.matmul(qkb[:, 0, :], xT[:, t % 2, c, :], wq[:, c, :],
                                                 start=(c == 0), stop=(c == ch - 1))
                        for c in range(ch):
                            mm = nc.tensor.matmul(qkb[0:rows, 1, :], xT[:, t % 2, c, 0:rows], kv[:, c, 0:D],
                                                  start=(c == 0), stop=(c == ch - 1))
                        mm.then_inc(qk_done.sem, 1)

                    def trqk(t):
                        rows = CL if t == QT else P
                        pe.wait_ge(qkn_ready.sem, qkn_ready.have(b, t))
                        pe.wait_ge(low_ready.sem, low_ready.back(b, t, 1))
                        if t < QT:
                            for c in range(DC):
                                nc.tensor.transpose(tqb[:, c * P:c * P + P], qkn[:, t % 2, c * P:c * P + P], k.ident[:, :])
                        for c in range(DC):
                            mm = nc.tensor.transpose(tkb[:, c * P:c * P + rows],
                                                     qkn[0:rows, t % 2, D + c * P:D + c * P + P], k.ident[0:rows, 0:rows])
                        mm.then_inc(tqk_done.sem, 1)

                    pe.wait_ge(x1_ready.sem, x1_ready.back(b, QT - 1, QT))
                    for s in range(QT + 3):
                        if s <= QT:
                            tr(s)
                        if 1 <= s <= QT + 1:
                            proj(s - 1)
                        if s >= 2:
                            trqk(s - 2)
                    pe.wait_ge(low_ready.sem, low_ready.have(b, QT))
                    pe.wait_ge(v_copied.sem, v_copied.have(b, QT))

                    def scores(n):
                        h, qt = n // QT, n % QT
                        pe.wait_ge(exp_done.sem, exp_done.back(b, n, 2))
                        q = Q2[:, h, qt * P:qt * P + P]
                        for a, z in ((0, S), (S, KEYS)):
                            nc.tensor.matmul(Sb[n % 2][:, a:z], q, KH[:, h, a:z], start=True, stop=False)
                            nc.tensor.matmul(Sb[n % 2][:, a:z], q, KL[:, h, a:z], start=False, stop=(a == 0))
                        nc.tensor.matmul(Sb[n % 2][:, S:KEYS], one_row[:, :], mrow[0:1, ds(b, 1), :]
                                         .rearrange("o a n -> o (a n)"), start=False, stop=True).then_inc(s_done.sem, 1)

                    def turn(n):
                        h, qt = n // QT, n % QT
                        pe.wait_ge(p_ready.sem, p_ready.have(b, n))
                        pe.wait_ge(ptm_out.sem, ptm_out.back(b, n, 2))
                        if qt == 0:
                            pe.wait_ge(ptc_out.sem, ptc_out.back(b, h, 1))
                        for c in range(QT):
                            nc.tensor.transpose(ptm[n % 2][:, c * P:c * P + P], Pr[:, n % PRING, c * P:c * P + P],
                                                k.ident[:, :])
                        nc.tensor.transpose(ptc[0:CL, qt * P:qt * P + P], Pr[:, n % PRING, S:KEYS], k.ident[:, :])\
                            .then_inc(t_done.sem, 1)

                    def pv(g):
                        pe.wait_ge(ptm_out.sem, ptm_out.have(b, 2 * QT * g + 2 * QT - 1))
                        pe.wait_ge(ptc_out.sem, ptc_out.have(b, 2 * g + 1))
                        pe.wait_ge(ot_out.sem, ot_out.back(b, g, 1))
                        for c in range(QT + 1):
                            rows = CL if c == QT else P
                            for r in range(2):
                                h = 2 * g + r
                                mm = nc.tensor.matmul(otb[DH0 * r:DH0 * r + DH0, :], V[0:rows, c, DH0 * h:DH0 * h + DH0],
                                                      PT[0:rows, r, c, :], start=(c == 0), stop=(c == QT))
                        mm.then_inc(pv_done.sem, 1)

                    for n in range(U0 + 3):
                        if n < U0:
                            scores(n)
                        if n >= 10 and (n - 10) % 8 == 0:
                            pv((n - 10) // 8)
                        if 2 <= n < U0 + 2:
                            turn(n - 2)
                    pe.wait_ge(ot_out.sem, ot_out.have(b, 3))
                    for qt in range(QT):
                        for c in range(DC):
                            mm = nc.tensor.matmul(bank[:, qt, :], OT[:, c, qt * P:qt * P + P], wo[:, c, :],
                                                  start=(c == 0), stop=(c == DC - 1))
                        mm.then_inc(wo_done.sem, 1)

                rounds(pe, body)

            @block.scalar
            def _(act):
                credit(act, xT_ready, v_copied, exp_done, ptm_out, ot_out)
                act.wait_ge(folded, 3)

                def body(b, more):
                    for s in range(QT + 3):
                        if s <= QT:
                            t = s
                            rows, ch, g_, b_ = (CL, CC, lxg, lxb) if t == QT else (P, DC, lng, lnb)
                            act.wait_ge(y_read.sem, y_read.have(b, t))
                            act.wait_ge(qk_done.sem, qk_done.back(b, t, 2))
                            for c in range(ch):
                                i = act.activation(xT[:, t % 2, c, 0:rows], trb[:, c * P:c * P + rows],
                                                   ACT.Identity, bias=b_[:, c:c + 1], scale=g_[:, c:c + 1])
                            i.then_inc(xT_ready.sem, 1)
                        if 1 <= s <= QT + 1:
                            t = s - 1
                            rows, c0 = (CL, D) if t == QT else (P, 0)
                            act.wait_ge(v_done.sem, v_done.have(b, t))
                            act.activation(V[0:rows, t, :], vb[0:rows, :], ACT.Copy).then_inc(v_copied.sem, 1)
                            act.wait_ge(qk_done.sem, qk_done.have(b, t))
                            act.wait_ge(ss_done.sem, ss_done.back(b, t, 1))
                            act.activation(sq[0:rows, c0:], qkbs[t % 2][0:rows, :, :].rearrange("p a n -> p (a n)")[:, c0:],
                                           ACT.Square).then_inc(squared.sem, 1)
                        if s >= 2:
                            t = s - 2
                            rows = CL if t == QT else P
                            act.wait_ge(tqk_done.sem, tqk_done.have(b, t))
                            for par in range(2):
                                own, other = slice(DH0 * par, DH0 * par + DH0), slice(DH0 - DH0 * par, P - DH0 * par)
                                if t < QT:
                                    act.activation(Q2[own, par::2, t * P:t * P + P], chunks(tqb)[own, :, :], ACT.Copy,
                                                   scale=qgain[own, 0:1])
                                for to in (own, other):
                                    i = act.activation(KH[to, par::2, t * P:t * P + rows], chunks(tkb)[own, :, 0:rows],
                                                       ACT.Copy)
                            i.then_inc(high_ready.sem, 1)

                    for n in range(U0 + 4):
                        if 3 <= n < U0 + 3:
                            m = n - 3
                            h, qt = m // QT, m % QT
                            act.wait_ge(t_done.sem, t_done.have(b, m))
                            if h % 2 == 0 and qt == 0:
                                act.wait_ge(pv_done.sem, pv_done.back(b, h // 2, 1))
                            act.activation(PT[:, h % 2, 0:QT, qt * P:qt * P + P],
                                           ptm[m % 2].rearrange("p (c n) -> p c n", c=QT), ACT.Copy)\
                                .then_inc(ptm_out.sem, 1)
                        if n < U0:
                            act.wait_ge(max_done.sem, max_done.have(b, n))
                            act.wait_ge(t_done.sem, t_done.back(b, n, PRING))
                            act.activation(Pr[:, n % PRING, :], Sb[n % 2][:, 0:KEYS], ACT.Exp,
                                           bias=nmax[:, n % 4:n % 4 + 1],
                                           accum_out=rsum[:, n % 4:n % 4 + 1]).then_inc(exp_done.sem, 1)
                        if n >= 11 and (n - 11) % 8 == 0:
                            g_ = (n - 11) // 8
                            act.wait_ge(pv_done.sem, pv_done.have(b, g_))
                            act.activation(OT[:, g_, :], otb, ACT.Copy).then_inc(ot_out.sem, 1)

                rounds(act, body)

            @block.vector
            def _(dve):
                credit(dve, ss_done, qkn_ready, low_ready, ptc_out, x1_ready)

                def ln_piece(b, piece):
                    kind, t = piece
                    rows, x, y = (CL, XC[0:CL, :], YC[0:CL, :]) if t == QT else (P, X[:, t, :], Y[:, t, :])
                    chain = [q for q in LN_PIECES[:LN_PIECES.index(piece)]]
                    step = sum(1 if q[0] == "a" else (2 if q[0] == "b" and q[1] < QT else 0) for q in chain)

                    def stats(src, step):
                        n = LN_STATS.index(piece)
                        dve.bn_stats(bst[0:rows, n, :], src).then_inc(ln_step.sem, 1)
                        dve.wait_ge(ln_step.sem, ln_step.have(b, step))
                        dve.nop(nofuse=True)
                        dve.bn_aggr(mv[0:rows, n, :], bst[0:rows, n, :]).then_inc(stat.sem, 1)

                    def normalise(dst, src, n):
                        dve.wait_ge(rst.sem, rst.have(b, n))
                        return dve.tensor_scalar(dst, src, mv[0:rows, n, 0:1], rstd[0:rows, n:n + 1],
                                                 ALU.subtract, ALU.mult)
                    if kind == "a":
                        dve.wait_ge(x_in[t], b * 16 + 16)
                        stats(x, step)
                    elif kind == "b":
                        dve.wait_ge(y_read.sem, y_read.back(b, t, 5))
                        i = normalise(y, x, LN_STATS.index(("a", t)))
                        if t == QT:
                            i.then_inc(y_ready.sem, 1)
                            dve.wait_ge(y_ready.sem, y_ready.have(b, 4))
                            dve.sem_inc(x_free.sem, 1)
                        else:
                            i.then_inc(ln_step.sem, 1)
                            dve.wait_ge(ln_step.sem, ln_step.have(b, step))
                            dve.sem_inc(x_free.sem, 1)
                            stats(y, step + 1)
                    else:
                        normalise(y, y, LN_STATS.index(("b", t))).then_inc(y_ready.sem, 1)

                for piece in LN_PIECES:
                    ln_piece(0, piece)

                def body(b, more):
                    for s in range(1, QT + 3):
                        if s <= QT + 1:
                            t = s - 1
                            rows, h0 = (CL, H0) if t == QT else (P, 0)
                            dve.wait_ge(squared.sem, squared.have(b, t))
                            dve.wait_ge(rn_done.sem, rn_done.back(b, t, 1))
                            dve.tensor_reduce(ss[0:rows, h0:], sq[0:rows, h0 * DH0:].rearrange("p (h d) -> p h d", d=DH0),
                                              AX.X, ALU.add).then_inc(ss_done.sem, 1)
                            dve.wait_ge(rn_done.sem, rn_done.have(b, t))
                            dve.wait_ge(tqk_done.sem, tqk_done.back(b, t, 2))
                            dve.tensor_tensor(
                                qkn[0:rows, t % 2, h0 * DH0:].rearrange("p (h d) -> p h d", d=DH0),
                                qkbs[t % 2][0:rows, :, :].rearrange("p a n -> p (a n)")[:, h0 * DH0:]
                                .rearrange("p (h d) -> p h d", d=DH0),
                                rn[0:rows, h0:].unsqueeze(2).to_broadcast([rows, 2 * H0 - h0, DH0]), ALU.mult)\
                                .then_inc(qkn_ready.sem, 1)
                        if s >= 2:
                            t = s - 2
                            rows = CL if t == QT else P
                            dve.wait_ge(high_ready.sem, high_ready.have(b, t))
                            for par in range(2):
                                own, other = slice(DH0 * par, DH0 * par + DH0), slice(DH0 - DH0 * par, P - DH0 * par)
                                if t < QT:
                                    cols = slice(t * P, t * P + P)
                                    dve.scalar_tensor_tensor(Q2[other, par::2, cols], chunks(tqb)[own, :, :],
                                                             qgain[own, 0:1], Q2[own, par::2, cols].bitcast(F32),
                                                             ALU.mult, ALU.subtract)
                                cols = slice(t * P, t * P + rows)
                                for to in (own, other):
                                    i = dve.tensor_tensor(KL[to, par::2, cols], chunks(tkb)[own, :, 0:rows],
                                                          KH[own, par::2, cols].bitcast(F32), ALU.subtract)
                            i.then_inc(low_ready.sem, 1)

                    for n in range(U0 + 3):
                        if n >= 6 and (n - 6) % 4 == 0:
                            h = (n - 6) // 4
                            dve.wait_ge(t_done.sem, t_done.have(b, QT * h + 3))
                            dve.wait_ge(pv_done.sem, pv_done.back(b, h // 2, 1))
                            dve.tensor_copy(PT[0:CL, h % 2, QT, :], ptc[0:CL, :]).then_inc(ptc_out.sem, 1)
                        if n < U0:
                            dve.wait_ge(s_done.sem, s_done.have(b, n))
                            dve.tensor_reduce(nmax[:, n % 4:n % 4 + 1], Sb[n % 2][:, 0:KEYS], AX.X, ALU.max, negate=True)\
                                .then_inc(max_done.sem, 1)
                        if 1 <= n <= U0:
                            m = n - 1
                            dve.wait_ge(exp_done.sem, exp_done.have(b, m))
                            dve.reciprocal(rinv[:, m % 4:m % 4 + 1], rsum[:, m % 4:m % 4 + 1]).then_inc(rinv_step.sem, 1)
                            dve.wait_ge(rinv_step.sem, rinv_step.have(b, m))
                            dve.tensor_scalar(Pr[:, m % PRING, :], Pr[:, m % PRING, :], rinv[:, m % 4:m % 4 + 1], None,
                                              ALU.mult).then_inc(p_ready.sem, 1)
                        if more and n % 2 == 0 and n // 2 < len(LN_PIECES):
                            ln_piece(b + 1, LN_PIECES[n // 2])
                    for qt in range(QT):
                        dve.wait_ge(wo_done.sem, wo_done.have(b, qt))
                        dve.wait_ge(r_biased.sem, r_biased.have(b, qt))
                        dve.scalar_tensor_tensor(R[:, qt, :], bank[:, qt, :], k.gate[:, 0:1], R[:, qt, :],
                                                 ALU.mult, ALU.add).then_inc(x1_ready.sem, 1)

                rounds(dve, body)
    sems.give_back()


def route(nc, k, name, onehot, na, nt, slot_i, idx_i, te_i):
    nh = nt * ROWS // P
    with ExitStack() as ctx:
        sb = lambda n, s, d=F32: ctx.enter_context(nc.sbuf_tensor(name + n, s, d))
        sem = lambda n: k.sems.enter_context(nc.semaphore(name + n))
        tot, inc, off = sb("tot", [P, E, na]), sb("inc", [P, E, na]), sb("off", [P, E, na])
        cnt, cnt_i = sb("cnt", [P, E]), sb("cnt_i", [P, E], I32)
        tiles, tinc, base = sb("tiles", [P, E]), sb("tinc", [P, E]), sb("base", [P, E])
        slot, lo_i, hi_i = sb("slot", [P, na]), sb("lo_i", [P, na], I32), sb("hi_i", [P, na], I32)
        lo, hi = sb("lo", [P, na]), sb("hi", [P, na])
        iota_h, te = sb("iota_h", [P, nh]), sb("te", [P, nt])
        RING = 4
        oh_lo, oh_hi = sb("oh_lo", [P, RING, P]), sb("oh_hi", [P, RING, nh])
        one_na = sb("one_na", [P, na])
        pre_b, tot_b = k.bank[:, 0, 0:E * na], k.bank[:, 1, 0:E * na]
        inv_b = k.bank[:, 2, 0:nh]
        step, made, counted = sem("step"), sem("made"), sem("counted")
        built, used, inverted = sem("built"), sem("used"), sem("inverted")

        with nc.Block() as block:
            @block.gpsimd
            def _(pool):
                pool.iota(iota_h[:, :], [[1, nh]], base=0, channel_multiplier=0,
                          allow_small_or_imprecise_dtypes=True).then_inc(made, 1)
                pool.memset(one_na[:, :], 1.0).then_inc(made, 1)
                pool.wait_ge(made, 2)

            @block.tensor
            def _(pe):
                flat = onehot.rearrange("p e a -> p (e a)")
                nc.tensor.matmul(pre_b, k.tri[:, :], flat, start=True, stop=True)
                nc.tensor.matmul(tot_b, k.ones[:, :], flat, start=True, stop=True).then_inc(counted, 1)

                def invert(a, first, last, n0):
                    for q in range(RING):
                        pe.wait_ge(built, n0 + q + 1)
                        nc.tensor.matmul(inv_b, oh_lo[:, q, :], oh_hi[:, q, :], start=(first and q == 0),
                                         stop=(last and q == RING - 1), skip_group_check=True).then_inc(used, 1)
                invert(0, True, False, 0)
                with pe.Fori(1, na // RING - 1) as g:
                    invert(g, False, False, g * RING)
                invert(0, False, True, na - RING)

            @block.vector
            def _(dve):
                n = [0]

                def then(ins):
                    n[0] += 1
                    ins.then_inc(step, 1)
                    dve.wait_ge(step, n[0])

                dve.wait_ge(made, 2)
                dve.wait_ge(counted, 1)
                then(dve.tensor_copy(tot[:, :, :], tot_b.rearrange("p (e a) -> p e a", e=E)))
                for e in range(E):
                    then(dve.tensor_tensor_scan(inc[:, e, :], one_na[:, :], tot[:, e, :], 0.0, ALU.mult, ALU.add))
                then(dve.tensor_scalar(cnt_i[:, :], inc[:, :, na - 1], float(ROWS - 1), None, ALU.add))
                then(dve.tensor_scalar(cnt_i[:, :], cnt_i[:, :], ROWS.bit_length() - 1, None, ALU.logical_shift_right))
                then(dve.tensor_copy(tiles[:, :], cnt_i[:, :]))
                then(dve.tensor_tensor_scan(tinc[:, :], one_na[:, 0:E], tiles[:, :], 0.0, ALU.mult, ALU.add))
                then(dve.tensor_tensor(base[:, :], tinc[:, :], tiles[:, :], ALU.subtract))
                then(dve.tensor_scalar(base[:, :], base[:, :], float(ROWS), None, ALU.mult))
                then(dve.tensor_tensor(off[:, :, :], inc[:, :, :], tot[:, :, :], ALU.subtract))
                then(dve.tensor_tensor(off[:, :, :], off[:, :, :], pre_b.rearrange("p (e a) -> p e a", e=E), ALU.add))
                then(dve.tensor_tensor(off[:, :, :], off[:, :, :], base[:, :].unsqueeze(2).to_broadcast([P, E, na]), ALU.add))
                then(dve.tensor_tensor(off[:, :, :], off[:, :, :], onehot, ALU.mult))
                then(dve.tensor_reduce(slot[:, :], off[:, :, :].rearrange("p e a -> p a e"), AX.X, ALU.add))
                then(dve.tensor_copy(slot_i, slot[:, :]))
                then(dve.tensor_scalar(lo_i[:, :], slot_i, P - 1, None, ALU.bitwise_and))
                then(dve.tensor_scalar(hi_i[:, :], slot_i, P.bit_length() - 1, None, ALU.logical_shift_right))
                then(dve.tensor_copy(lo[:, :], lo_i[:, :]))
                then(dve.tensor_copy(hi[:, :], hi_i[:, :]))
                then(dve.tensor_scalar(te[:, :], iota_h[:, 0:nt], tinc[:, 0:1], None, ALU.is_ge))
                for e in range(1, E):
                    then(dve.scalar_tensor_tensor(te[:, :], iota_h[:, 0:nt], tinc[:, e:e + 1], te[:, :], ALU.is_ge, ALU.add))
                then(dve.tensor_scalar(te[:, :], te[:, :], float(E - 1), None, ALU.min))
                then(dve.tensor_copy(te_i, te[0:1, :]))
                na2 = na // 2

                def pair(a, tok, q):
                    dve.tensor_scalar(oh_lo[:, q, :], k.iota_p[:, :], lo[:, ds(a, 1)], None, ALU.is_equal)
                    dve.tensor_scalar(oh_hi[:, q, :], iota_h[:, :], hi[:, ds(a, 1)], k.tokcol[:, ds(tok, 1)],
                                      ALU.is_equal, ALU.mult).then_inc(built, 1)
                for q in range(RING):
                    pair(q, q, q)
                with dve.Fori(1, na2 // RING) as g:
                    for q in range(RING):
                        dve.wait_ge(used, (g - 1) * RING + q + 1)
                        pair(g * RING + q, g * RING + q, q)
                with dve.Fori(0, na2 // RING) as g:
                    for q in range(RING):
                        dve.wait_ge(used, na2 - RING + g * RING + q + 1)
                        pair(na2 + g * RING + q, g * RING + q, q)
                dve.wait_ge(used, na)
                then(dve.tensor_copy(idx_i, inv_b))


def route_given(nc, k, ins):
    with ExitStack() as ctx:
        sb = lambda n, s, d=F32: ctx.enter_context(nc.sbuf_tensor("rg_" + n, s, d))
        sem = lambda n: k.sems.enter_context(nc.semaphore("rg_" + n))
        ei, ef, oh = sb("ei", [P, NA0], I32), sb("ef", [P, NA0]), sb("oh", [P, E, NA0])
        ew, loaded, step = sb("ew", [P, NA0]), sem("loaded"), sem("step")
        with nc.Block() as block:
            @block.sync
            def _(sp):
                sp.dma_start(ei[:, :], ins["ei"]).then_inc(loaded, 16)
                sp.dma_start(ew[:, :], ins["ew"]).then_inc(loaded, 16)

            @block.vector
            def _(dve):
                dve.wait_ge(loaded, 32)
                dve.tensor_copy(ef[:, :], ei[:, :]).then_inc(step, 1)
                dve.wait_ge(step, 1)
                dve.tensor_tensor(oh[:, :, :], ef[:, :].unsqueeze(1).to_broadcast([P, E, NA0]),
                                  k.iota_e[:, :].unsqueeze(2).to_broadcast([P, E, NA0]), ALU.is_equal).then_inc(step, 1)
                dve.tensor_scalar(k.w0[:, :], ew[:, :], k.gate[:, 2:3], None, ALU.mult).then_inc(step, 1)
                dve.wait_ge(step, 3)
        route(nc, k, "r0_", oh[:, :, :], NA0, NT0, k.slot0[:, :], k.idx0[:, :], k.te0[:, :])


def route_top2(nc, k):
    NT = B * QT
    with ExitStack() as ctx:
        sb = lambda n, s, d=F32: ctx.enter_context(nc.sbuf_tensor("rt_" + n, s, d))
        sem = lambda n: k.sems.enter_context(nc.semaphore("rt_" + n))
        pr, m, r = sb("pr", [P, NT, E]), sb("m", [P, NT]), sb("r", [P, NT])
        rank, cand, c1, oh = sb("rank", [P, E]), sb("cand", [P, NT, E]), sb("c1", [P, NT]), sb("oh", [P, E, NA1])
        top = sb("top", [P, NA1])
        step, expd = sem("step"), sem("expd")
        centred = sem("centred")
        wide = lambda v: v.unsqueeze(2).to_broadcast([P, NT, E])
        with nc.Block() as block:
            @block.scalar
            def _(act):
                act.wait_ge(centred, 1)
                act.activation(pr[:, :, :], pr[:, :, :], ACT.Exp).then_inc(expd, 1)

            @block.vector
            def _(dve):
                n = [0]

                def then(ins):
                    n[0] += 1
                    ins.then_inc(step, 1)
                    dve.wait_ge(step, n[0])

                then(dve.tensor_reduce(m[:, :], k.logits[:, :, :], AX.X, ALU.max))
                dve.tensor_tensor(pr[:, :, :], k.logits[:, :, :], wide(m[:, :]), ALU.subtract).then_inc(centred, 1)
                then(dve.tensor_scalar(rank[:, :], k.iota_e[:, :], -1.0, float(E), ALU.mult, ALU.add))
                dve.wait_ge(expd, 1)
                then(dve.tensor_reduce(m[:, :], pr[:, :, :], AX.X, ALU.add))
                then(dve.reciprocal(r[:, :], m[:, :]))
                then(dve.tensor_tensor(pr[:, :, :], pr[:, :, :], wide(r[:, :]), ALU.mult))
                for c in range(2):
                    t = top[:, c * NT:c * NT + NT]
                    hot = oh[:, :, c * NT:c * NT + NT].rearrange("p e t -> p t e")
                    rk = rank[:, :].unsqueeze(1).to_broadcast([P, NT, E])
                    then(dve.tensor_reduce(t, pr[:, :, :], AX.X, ALU.max))
                    then(dve.tensor_tensor(cand[:, :, :], pr[:, :, :], wide(t), ALU.is_equal))
                    then(dve.tensor_tensor(cand[:, :, :], cand[:, :, :], rk, ALU.mult))
                    then(dve.tensor_reduce(c1[:, :], cand[:, :, :], AX.X, ALU.max))
                    then(dve.tensor_tensor(cand[:, :, :], rk, wide(c1[:, :]), ALU.is_equal))
                    then(dve.tensor_copy(hot, cand[:, :, :]))
                    if c == 0:
                        then(dve.scalar_tensor_tensor(pr[:, :, :], cand[:, :, :], -2.0, pr[:, :, :], ALU.mult, ALU.add))
                then(dve.tensor_scalar(k.w1[:, :], top[:, :], k.gate[:, 3:4], None, ALU.mult))
        route(nc, k, "r1_", oh[:, :, :], NA1, NT1, k.slot1[:, :], k.idx1[:, :], k.te1[:, :])


def experts(nc, k, name, src, w_up, w_gate, w_down, ff, nt, idx_i, te_i, dst):
    MT = ROWS // P
    FC = ff // P
    SLOTS = 8
    UP = 4
    DOWN = FC // 4
    PIECES = UP + DOWN
    PIECE = 4 * D
    gated = w_gate is not None
    fpp = ff // UP
    assert SLOTS * (1 if gated else 2) == FC and PIECES % 2 == 0
    with ExitStack() as ctx:
        sb = lambda n, s, d=F32: ctx.enter_context(nc.sbuf_tensor(name + n, s, d))
        sem = lambda n: k.sems.enter_context(nc.semaphore(name + n))
        count = lambda n, per, credit=0: Count(k.sems, nc, name + n, per, credit)
        raw = sb("raw", [P, 2, PIECE])
        WH, WL = sb("WH", [P, PIECES, PIECE], F32R), sb("WL", [P, PIECES, PIECE], F32R)
        X, Yo = sb("X", [P, MT, D]), sb("Yo", [P, MT, D])
        xh, xl = sb("xh", [P, DC, ROWS], F32R), sb("xl", [P, DC, ROWS], F32R)
        HW = ROWS if gated else 2 * ROWS
        hh, hl = sb("hh", [P, SLOTS, HW], F32R), sb("hl", [P, SLOTS, HW], F32R)
        hf, sil = sb("hf", [P, 2, HW]), (sb("sil", [P, 2, ROWS]) if gated else None)
        icol = sb("icol", [P, MT], I32)
        bst, mv = sb("bst", [P, MT, 6]), sb("mv", [P, MT, 2])
        veps, rstd = sb("veps", [P, MT]), sb("rstd", [P, MT])
        RING = 4
        up = [k.bank[:, n, :] for n in (0, 1, 4, 5)]
        warm = sb("warm", [P, 2])
        down = [k.bank[:, 2, :], k.bank[:, 3, :]]
        trb = [k.bank[:, 6, :], k.bank[:, 7, :]]
        raw_in, x_in, y_out = [sem(f"raw_in{s}") for s in range(2)], [sem(f"x_in{m}") for m in range(MT)], sem("y_out")
        raw_step = (16 if not gated else 32)
        raw_round = UP // 2 * raw_step + DOWN // 2 * 16
        icopied = count("icopied", 1)
        stepped, stat, rst = count("bn_step", MT), count("stat", MT), count("rstd_ready", 1)
        veps_step = count("veps_step", 1)
        x_ready, x_read = count("x_ready", MT), count("x_read", MT, MT)
        xh_step, xT_ready = count("xh_step", MT), count("xT_ready", MT, MT)
        up_done, act_done = count("up_done", SLOTS), count("act_done", SLOTS, 0 if gated else RING)
        warmed = sem("warmed")
        hf_ready, hh_step, h_ready = count("hf_ready", SLOTS, RING), count("hh_step", SLOTS), count("h_ready", SLOTS, 2)
        high_ready, w_ready = count("high_ready", PIECES), count("w_ready", PIECES, 2)
        down_done, y_ready = count("down_done", DOWN), count("y_ready", MT, MT)

        bank_read = hf_ready if gated else act_done

        def tiles(eng, body):
            with eng.Fori(0, nt - 1) as j:
                body(j, True)
            body(nt - 1, False)

        def cols(w, p):
            return w[:, p, :].rearrange("p (g c n) -> p g c n", g=2 if gated else 1, c=DC)

        with nc.Block() as block:
            @block.sync
            def _(sp):
                def load(j):
                    e = sp.value_load(te_i[0:1, ds(j, 1)], min_val=0, max_val=E - 1)
                    for p in range(PIECES):
                        sp.wait_ge(w_ready.sem, w_ready.back(j, p, 2))
                        sp.nop(nofuse=True)
                        if p < UP:
                            for g, w in enumerate((w_up, w_gate) if gated else (w_up,)):
                                sp.dma_start(cols(raw, p % 2)[:, g, :, :],
                                             w[ds(e, 1), :, fpp * p:fpp * p + fpp].rearrange("o (c p) n -> p (o c) n", p=P))\
                                    .then_inc(raw_in[p % 2], 16)
                        else:
                            q = p - UP
                            sp.dma_start(raw[:, p % 2, :].rearrange("p (c n) -> p c n", n=D),
                                         w_down[ds(e, 1), 4 * P * q:4 * P * (q + 1), :].rearrange("o (c p) n -> p (o c) n", p=P))\
                                .then_inc(raw_in[p % 2], 16)
                with sp.Fori(0, nt) as j:
                    load(j)

            @block.gpsimd
            def _(pool):
                def gather(j):
                    pool.wait_ge(x_read.sem, x_read.back(j, MT - 1, MT))
                    pool.tensor_copy(icol[:, :], idx_i[:, ds(j * MT, MT)]).then_inc(icopied.sem, 1)
                    pool.wait_ge(icopied.sem, icopied.have(j, 0))
                    pool.nop(nofuse=True)
                    for m in range(MT):
                        pool.indirect_dma_start(X[:, m, :], None, src, bass.IndirectOffsetOnAxis(icol[:, m:m + 1], 0))\
                            .then_inc(x_in[m], 16)
                    pool.wait_ge(stat.sem, stat.have(j, MT - 1))
                    pool.nop(nofuse=True)
                    pool.tensor_scalar(veps[:, :], mv[:, :, 1], EPS, None, ALU.add).then_inc(veps_step.sem, 1)
                    pool.wait_ge(veps_step.sem, veps_step.have(j, 0))
                    pool.tensor_tensor(rstd[:, :], veps[:, :], k.halfneg[:, 0:MT], ALU.pow).then_inc(rst.sem, 1)

                with pool.Fori(0, nt) as j:
                    gather(j)

            @block.tensor
            def _(pe):
                pe.sem_inc(x_read.sem, x_read.credit)

                def turn(j):
                    for m in range(MT):
                        pe.wait_ge(x_ready.sem, x_ready.have(j, m))
                        pe.wait_ge(xT_ready.sem, xT_ready.back(j, m, MT))
                        for c in range(DC):
                            mm = nc.tensor.transpose(trb[m][:, c * P:c * P + P], X[:, m, c * P:c * P + P], k.ident[:, :])
                        mm.then_inc(x_read.sem, 1)

                turn(0)

                def body(j, more):
                    pe.wait_ge(xT_ready.sem, xT_ready.have(j, MT - 1))
                    for n in range(SLOTS):
                        pc = n // 2
                        if n % 2 == 0:
                            pe.wait_ge(w_ready.sem, w_ready.have(j, pc))
                        pe.wait_ge(bank_read.sem, bank_read.back(j, n, RING))
                        for q in range(2):
                            g, f = (q, n % 2) if gated else (0, 2 * (n % 2) + q)
                            for c in range(DC):
                                high, low = (cols(w, pc)[:, g, c, f * P:f * P + P] for w in (WH, WL))
                                for i, (w, x) in enumerate(((high, xh), (high, xl), (low, xh))):
                                    mm = nc.tensor.matmul(up[n % RING][:, q * ROWS:q * ROWS + ROWS], w, x[:, c, :],
                                                          start=(c == 0 and i == 0), stop=(c == DC - 1 and i == 2))
                        mm.then_inc(up_done.sem, 1)
                    if more:
                        turn(j + 1)
                    pe.wait_ge(y_ready.sem, y_ready.back(j, MT - 1, MT))
                    for pc in range(UP, PIECES):
                        pe.wait_ge(w_ready.sem, w_ready.have(j, pc))
                        for q in range(4):
                            f = 4 * (pc - UP) + q
                            n, o = (f, 0) if gated else (f // 2, f % 2 * ROWS)
                            pe.wait_ge(h_ready.sem, h_ready.have(j, n))
                            for m in range(MT):
                                high, low = (h[:, n, o + m * P:o + m * P + P] for h in (hh, hl))
                                wh, wl = (w[:, pc, q * D:q * D + D] for w in (WH, WL))
                                for i, (h, w) in enumerate(((high, wh), (high, wl), (low, wh))):
                                    mm = nc.tensor.matmul(down[m], h, w, start=(f == 0 and i == 0),
                                                          stop=(f == FC - 1 and i == 2))
                        mm.then_inc(down_done.sem, 1)
                tiles(pe, body)

            @block.scalar
            def _(act):
                act.sem_inc(y_ready.sem, y_ready.credit)
                act.sem_inc(y_out, 16)
                if not gated:
                    act.sem_inc(act_done.sem, act_done.credit)

                def split(j, p, first=False):
                    if not first:
                        if p < UP:
                            act.wait_ge(up_done.sem, up_done.have(j, 2 * p + 1) - SLOTS)
                        else:
                            act.wait_ge(down_done.sem, down_done.have(j, p - UP) - DOWN)
                    s, a = p % 2, p // 2 + 1
                    here = min(a, UP // 2) * raw_step + max(a - UP // 2, 0) * 16
                    act.wait_ge(raw_in[s], j * raw_round + here)
                    act.activation(WH[:, p, :], raw[:, s, :], ACT.Copy).then_inc(high_ready.sem, 1)

                for p in range(PIECES):
                    split(0, p, True)
                act.wait_ge(warmed, 1)

                def body(j, more):
                    act.activation(warm[:, 1:2], warm[:, 0:1], ACT.Silu if gated else ACT.Gelu)
                    for n in range(SLOTS):
                        act.wait_ge(up_done.sem, up_done.have(j, n))
                        used = hf_ready if gated else h_ready
                        act.wait_ge(used.sem, used.back(j, n, 2))
                        if gated:
                            act.activation(sil[:, n % 2, :], up[n % RING][:, 0:ROWS], ACT.Silu).then_inc(act_done.sem, 1)
                        else:
                            act.activation(hf[:, n % 2, :], up[n % RING], ACT.Gelu).then_inc(act_done.sem, 1)
                        if more and n % 2 == 1:
                            split(j + 1, n // 2)
                    if more:
                        for p in range(UP, PIECES):
                            split(j + 1, p)
                    act.wait_ge(y_out, j * 16 + 16)
                    act.wait_ge(down_done.sem, down_done.have(j, DOWN - 1))
                    for m in range(MT):
                        act.activation(Yo[:, m, :], down[m], ACT.Copy).then_inc(y_ready.sem, 1)
                    act.wait_ge(y_ready.sem, y_ready.have(j, MT - 1))
                    act.dma_start(dst[ds(j * ROWS, ROWS), :].rearrange("(m p) n -> p m n", p=P), Yo[:, :, :])\
                        .then_inc(y_out, 16)
                tiles(act, body)
                act.wait_ge(y_out, 16 * (nt + 1))

            @block.vector
            def _(dve):
                for c in (xT_ready, h_ready, w_ready, hf_ready):
                    dve.sem_inc(c.sem, c.credit)
                dve.memset(warm[:, :], 0.0).then_inc(warmed, 1)

                def split(j, p):
                    dve.wait_ge(high_ready.sem, high_ready.have(j, p))
                    dve.tensor_tensor(WL[:, p, :], raw[:, p % 2, :], WH[:, p, :].bitcast(F32), ALU.subtract)\
                        .then_inc(w_ready.sem, 1)

                def norm(j):
                    for m in range(MT):
                        dve.wait_ge(x_in[m], j * 16 + 16)
                        dve.bn_stats(bst[:, m, :], X[:, m, :]).then_inc(stepped.sem, 1)
                    for m in range(MT):
                        dve.wait_ge(stepped.sem, stepped.have(j, m))
                        dve.nop(nofuse=True)
                        dve.bn_aggr(mv[:, m, :], bst[:, m, :]).then_inc(stat.sem, 1)

                def scale(j):
                    dve.wait_ge(rst.sem, rst.have(j, 0))
                    for m in range(MT):
                        dve.tensor_scalar(X[:, m, :], X[:, m, :], mv[:, m, 0:1], rstd[:, m:m + 1],
                                          ALU.subtract, ALU.mult).then_inc(x_ready.sem, 1)

                def columns(j):
                    for m in range(MT):
                        c = slice(m * P, m * P + P)
                        dve.wait_ge(x_read.sem, x_read.have(j, m))
                        dve.tensor_copy(xh[:, :, c], trb[m].rearrange("p (c n) -> p c n", c=DC)).then_inc(xh_step.sem, 1)
                        dve.wait_ge(xh_step.sem, xh_step.have(j, m))
                        dve.tensor_tensor(xl[:, :, c], trb[m].rearrange("p (c n) -> p c n", c=DC), xh[:, :, c].bitcast(F32),
                                          ALU.subtract).then_inc(xT_ready.sem, 1)

                norm(0)
                scale(0)
                columns(0)
                for p in range(PIECES):
                    split(0, p)

                def body(j, more):
                    for n in range(SLOTS):
                        dve.wait_ge(act_done.sem, act_done.have(j, n))
                        if gated:
                            dve.wait_ge(h_ready.sem, h_ready.back(j, n, 2))
                            dve.tensor_tensor(hf[:, n % 2, :], up[n % RING][:, ROWS:2 * ROWS], sil[:, n % 2, :], ALU.mult)\
                                .then_inc(hf_ready.sem, 1)
                            dve.wait_ge(hf_ready.sem, hf_ready.have(j, n))
                        dve.tensor_copy(hh[:, n, :], hf[:, n % 2, :]).then_inc(hh_step.sem, 1)
                        dve.wait_ge(hh_step.sem, hh_step.have(j, n))
                        dve.tensor_tensor(hl[:, n, :], hf[:, n % 2, :], hh[:, n, :].bitcast(F32), ALU.subtract)\
                            .then_inc(h_ready.sem, 1)
                        if more and n % 2 == 1:
                            split(j + 1, n // 2)
                        if more and n == 2:
                            norm(j + 1)
                        if more and n == 4:
                            scale(j + 1)
                    if more:
                        columns(j + 1)
                        for p in range(UP, PIECES):
                            split(j + 1, p)
                tiles(dve, body)


H1 = 16
DH1 = D // H1
HH = H1 // 2
U1 = 2 * QT


def attention1(nc, k, ins):
    with ExitStack() as ctx:
        sb = lambda n, s, d=F32: ctx.enter_context(nc.sbuf_tensor("a1_" + n, s, d))
        sem = lambda n: k.sems.enter_context(nc.semaphore("a1_" + n))
        count = lambda n, per, credit=0: Count(k.sems, nc, "a1_" + n, per, credit)
        wq, wk, wv, wo = sb("wq", [P, DC, D]), sb("wk", [P, CC, D]), sb("wv", [P, CC, D]), sb("wo", [P, DC, D])
        gw, ctxT = sb("gw", [P, DC, E]), sb("ctxT", [P, CC, B * CL])
        bq, bk = sb("bq", [P, DC]), sb("bk", [P, DC])
        bv, bo, bf = sb("bv", [P, D]), sb("bo", [P, D]), sb("bf", [P, D])
        kT, V = sb("kT", [P, DC, B * CL]), sb("V", [CL, B, H1, DH1 + 1])
        X, Y = sb("X", [P, QT, D]), sb("Y", [P, QT, D])
        G = sb("G", [P, 2, 2, D])
        icol, wcol = sb("icol", [P, 2, 2], I32), sb("wcol", [P, 2, 2])
        bst, mv = sb("bst", [P, QT, 6]), sb("mv", [P, QT, 2])
        veps, rstd = sb("veps", [P, QT]), sb("rstd", [P, QT])
        xT, qT = sb("xT", [P, DC, S]), sb("qT", [P, DC, S])
        Pr, PT = sb("Pr", [P, 2, HH, CL]), sb("PT", [CL, 2, HH, P])
        smax, rinv = sb("smax", [P, 2, HH]), sb("rinv", [P, 2, HH])
        O, OT = sb("O", [P, 2, D]), sb("OT", [P, 2, DC, P])
        R, N3, N3T = sb("R", [P, QT, D]), sb("N3", [P, 2, D]), sb("N3T", [P, 2, DC, P])
        bst3, mv3 = sb("bst3", [P, QT, 6]), sb("mv3", [P, QT, 2])
        veps3, rstd3 = sb("veps3", [P, QT]), sb("rstd3", [P, QT])
        bank = k.bank
        Sb = [bank[:, 2 * s:2 * s + 2, 0:4 * CL].rearrange("p g (h n) -> p g h n", h=4) for s in range(2)]
        tb = [bank[:, 4, :], bank[:, 5, :]]
        ob = bank[:, 6, 0:HH * (DH1 + 1)].rearrange("p (h d) -> p h d", h=HH)
        misc = bank[:, 7, :]

        w_in, folded = sem("weights_in"), sem("folded")
        vcur = sb("vcur", [CL, H1, DH1 + 1])
        kcur, kzeroed = sb("kcur", [P, H1, CL]), sem("kzeroed")
        k_ready, v_ready = count("k_ready", 1), count("v_ready", 1)
        kv_done, k_out, v_out = sem("kv_done"), sem("k_out"), sem("v_out")
        x_in, r_in = [sem(f"x_in{t}") for t in range(QT)], [sem(f"r_in{t}") for t in range(QT)]
        x2_out, x3_out = [sem(f"x2_out{t}") for t in range(QT)], [sem(f"x3_out{t}") for t in range(QT)]
        g_in = [[sem(f"g_in{s}{c}") for c in range(2)] for s in range(2)]
        icopied = count("icopied", QT)
        x_biased = count("x_biased", QT)
        summed, x2_ready = count("summed", QT), count("x2_ready", QT, 2)
        bn_step, stat, rst, veps_step = count("bn_step", QT), count("stat", QT), count("rst", QT), count("veps_step", QT)
        y_ready, y_read = count("y_ready", QT), count("y_read", QT, QT)
        xT_ready, q_done, qT_ready = count("xT_ready", QT), count("q_done", DC), count("qT_ready", DC)
        s_done, max_done = count("s_done", U1), count("max_done", U1)
        p_ready, exp_done = count("p_ready", U1, 2), count("exp_done", U1)
        t_done, pt_ready = count("t_done", 2 * U1, 4), count("pt_ready", 2 * U1, 2)
        pv_done, rinv_step, o_ready = count("pv_done", U1, 2), count("rinv_step", U1), count("o_ready", U1, 1)
        ot_done, ot_ready = count("ot_done", QT, 2), count("ot_ready", QT)
        wo_done, r_biased, x3_ready = count("wo_done", QT, 2), count("r_biased", QT), count("x3_ready", QT)
        bn3_step, stat3, rst3, veps3_step = count("bn3_step", QT), count("stat3", QT), count("rst3", QT), count("veps3_step", QT)
        n3_ready, n3_read, n3T_ready = count("n3_ready", QT, QT), count("n3_read", QT, 2), count("n3T_ready", QT)
        lg_done, lg_out = count("lg_done", QT, 2), count("lg_out", QT, QT)

        LAGS = (("o_turn", 4), ("out", 5), ("n_turn", 8), ("router", 9))
        MISC = [(kind, (u - lag) // 2) for u in range(U1 + 8) for kind, lag in LAGS
                if u >= lag and (u - lag) % 2 == 0 and (u - lag) // 2 < QT]

        def rounds(eng, body, tail):
            body(0, False, True)
            with eng.Fori(1, 3) as b:
                body(b, True, True)
            body(3, True, False)
            with eng.Fori(4, B - 1) as b:
                body(b, True, False)
            body(B - 1, True, None)
            tail(B - 1)

        def attend(b, prev, step, queries):
            for m in range(DC):
                if prev:
                    step(b - 1, U1 + m)
                queries(m)
            if prev:
                step(b - 1, U1 + 4)
            for u in range(U1):
                if prev and u < 3:
                    step(b - 1, U1 + 5 + u)
                step(b, u)

        def credit(eng, *counts):
            for c in counts:
                eng.sem_inc(c.sem, c.credit)

        with nc.Block() as block:
            @block.sync
            def _(sp):
                for dst, src in ((wq, "wq1"), (wk, "wk1"), (wv, "wv1"), (wo, "wo1"), (gw, "gw1"), (ctxT, "ctxT")):
                    sp.dma_start(dst[:, :, :], ins[src].rearrange("(c p) n -> p c n", p=P)).then_inc(w_in, 16)
                for dst, src in ((bq, "bq1"), (bk, "bk1")):
                    sp.dma_start(dst[:, :], ins[src]).then_inc(w_in, 16)
                for dst, src in ((bv, "bv1"), (bo, "bo1"), (bf, "bf0")):
                    sp.dma_start(dst[:, :], ins[src][None, :].to_broadcast([P, D])).then_inc(w_in, 16)

                def load_x(b, first):
                    for t in range(QT):
                        sp.wait_ge(x2_out[t], b * 16 + 16)
                        sp.nop(nofuse=True)
                        if not first:
                            sp.wait_ge(y_ready.sem, y_ready.have(b, t) - QT)
                            sp.nop(nofuse=True)
                        sp.dma_start(X[:, t, :], k.x1[ds(b * S + t * P, P), :]).then_inc(x_in[t], 16)

                def store_x2(b):
                    for t in range(QT):
                        sp.wait_ge(x2_ready.sem, x2_ready.have(b, t))
                        sp.dma_start(k.x2[ds(b * S + t * P, P), :], X[:, t, :]).then_inc(x2_out[t], 16)

                load_x(0, True)
                store_x2(0)

                def body(b, prev, succ):
                    if succ is not None:
                        load_x(b + 1, False)
                    for t in range(QT):
                        sp.wait_ge(x2_out[t], b * 16 + 32)
                        sp.nop(nofuse=True)
                        sp.wait_ge(x3_out[t], b * 16 + 16)
                        sp.nop(nofuse=True)
                        sp.wait_ge(n3_ready.sem, n3_ready.back(b, t, QT))
                        sp.nop(nofuse=True)
                        sp.dma_start(R[:, t, :], k.x2[ds(b * S + t * P, P), :]).then_inc(r_in[t], 16)
                    if succ is not None:
                        store_x2(b + 1)
                    for t in range(QT):
                        sp.wait_ge(x3_ready.sem, x3_ready.have(b, t))
                        sp.dma_start(k.x3[ds(b * S + t * P, P), :], R[:, t, :]).then_inc(x3_out[t], 16)
                rounds(sp, body, lambda b: None)
                for t in range(QT):
                    sp.wait_ge(x3_out[t], 16 * (B + 1))

            @block.gpsimd
            def _(pool):
                for t in range(QT):
                    pool.sem_inc(x2_out[t], 16)
                    pool.sem_inc(x3_out[t], 16)
                pool.wait_ge(w_in, 16 * 11)
                pool.tensor_scalar(bo[:, :], bo[:, :], k.gate[:, 1:2], None, ALU.mult).then_inc(folded, 1)
                pool.tensor_scalar(bf[:, :], bf[:, :], k.gate[:, 2:3], None, ALU.mult).then_inc(folded, 1)
                pool.memset(V[:, :, :, DH1:DH1 + 1], 1.0).then_inc(folded, 1)
                pool.memset(kcur[:, :, :], 0.0).then_inc(kzeroed, 1)
                pool.wait_ge(folded, 3)

                def prep(b, comb, between):
                    def fetch(t):
                        s = t % 2
                        pool.wait_ge(x2_ready.sem, x2_ready.back(b, t, 2))
                        for c in range(2):
                            pool.tensor_copy(icol[:, s, c:c + 1], k.slot0[:, ds(b * QT + (c * NA0 // 2 + t), 1)])
                            i = pool.tensor_copy(wcol[:, s, c:c + 1], k.w0[:, ds(b * QT + (c * NA0 // 2 + t), 1)])
                        i.then_inc(icopied.sem, 1)
                        pool.wait_ge(icopied.sem, icopied.have(b, t))
                        pool.nop(nofuse=True)
                        for c in range(2):
                            pool.indirect_dma_start(G[:, s, c, :], None, k.y0, bass.IndirectOffsetOnAxis(icol[:, s, c:c + 1], 0))\
                                .then_inc(g_in[s][c], 16)

                    def finish(t):
                        pool.wait_ge(stat.sem, stat.have(b, t))
                        pool.nop(nofuse=True)
                        pool.tensor_scalar(veps[:, t:t + 1], mv[:, t, 1:2], EPS, None, ALU.add).then_inc(veps_step.sem, 1)
                        pool.wait_ge(veps_step.sem, veps_step.have(b, t))
                        pool.tensor_tensor(rstd[:, t:t + 1], veps[:, t:t + 1], k.halfneg[:, 0:1], ALU.pow).then_inc(rst.sem, 1)

                    for t in range(QT):
                        pool.wait_ge(x_in[t], b * 16 + 16)
                        pool.tensor_tensor(X[:, t, :], X[:, t, :], bf[:, :], ALU.add).then_inc(x_biased.sem, 1)
                    if comb:
                        fetch(0)
                        fetch(1)
                    for t in range(QT):
                        finish(t)
                        if comb and t + 2 < QT:
                            fetch(t + 2)
                        between(t)

                pool.wait_ge(k_out, 2 * DC)
                pool.wait_ge(v_out, B)
                prep(0, True, lambda t: None)

                def rstd_x3(b, t):
                    pool.wait_ge(stat3.sem, stat3.have(b, t))
                    pool.nop(nofuse=True)
                    pool.tensor_scalar(veps3[:, t:t + 1], mv3[:, t, 1:2], EPS, None, ALU.add).then_inc(veps3_step.sem, 1)
                    pool.wait_ge(veps3_step.sem, veps3_step.have(b, t))
                    pool.tensor_tensor(rstd3[:, t:t + 1], veps3[:, t:t + 1], k.halfneg[:, 0:1], ALU.pow).then_inc(rst3.sem, 1)

                def body(b, prev, succ):
                    def residual(t):
                        pool.wait_ge(r_in[t], b * 16 + 16)
                        pool.tensor_tensor(R[:, t, :], R[:, t, :], bo[:, :], ALU.add).then_inc(r_biased.sem, 1)
                    if prev:
                        rstd_x3(b - 1, 2)
                    pool.wait_ge(pv_done.sem, pv_done.have(b, -1))
                    pool.tensor_copy(vcur[:, :, :], V[:, ds(b, 1), :, :].rearrange("p o h d -> p (o h) d")).then_inc(v_ready.sem, 1)
                    if prev:
                        rstd_x3(b - 1, 3)
                    if succ is None:
                        for t in range(QT):
                            residual(t)
                    else:
                        prep(b + 1, succ, residual)
                    rstd_x3(b, 0)
                    rstd_x3(b, 1)

                def tail(b):
                    rstd_x3(b, 2)
                    rstd_x3(b, 3)
                rounds(pool, body, tail)

            @block.tensor
            def _(pe):
                credit(pe, y_read, t_done, pv_done, ot_done, wo_done, n3_read, lg_done)
                pe.wait_ge(w_in, 16 * 11)
                pe.wait_ge(folded, 3)
                for n in range(2 * DC):
                    m, half = n // 2, n % 2
                    if n >= 2:
                        pe.wait_ge(k_out, n - 1)
                    for c in range(CC):
                        mm = nc.tensor.matmul(bank[:, n % 2, 0:4 * CL], wk[:, c, m * P:m * P + P],
                                              ctxT[:, c, half * 4 * CL:(half + 1) * 4 * CL], start=(c == 0), stop=(c == CC - 1))
                    mm.then_inc(kv_done, 1)
                for b in range(B):
                    if b >= 2:
                        pe.wait_ge(v_out, b - 1)
                    for c in range(CC):
                        mm = nc.tensor.matmul(bank[0:CL, 2 + b % 2, :], ctxT[:, c, b * CL:b * CL + CL], wv[:, c, :],
                                              start=(c == 0), stop=(c == CC - 1))
                    mm.then_inc(kv_done, 1)
                pe.wait_ge(k_out, 2 * DC)
                pe.wait_ge(v_out, B)

                def scores(b, u):
                    t, half = u // 2, u % 2
                    pe.wait_ge(p_ready.sem, p_ready.back(b, u, 2))
                    for c in range(DC):
                        h = 4 * c + 2 * half
                        mm = nc.tensor.matmul(Sb[half][:, c // 2, c % 2 * 2:c % 2 * 2 + 2, :], qT[:, c, t * P:t * P + P],
                                              kcur[:, h:h + 2, :], start=True, stop=True)
                    mm.then_inc(s_done.sem, 1)

                def turn(b, u):
                    pe.wait_ge(exp_done.sem, exp_done.have(b, u))
                    for q in range(2):
                        pe.wait_ge(pt_ready.sem, pt_ready.back(b, 2 * u + q, 2))
                        for i in range(4):
                            mm = nc.tensor.transpose(tb[q][0:CL, i * P:i * P + P], Pr[:, u % 2, 4 * q + i, :], k.ident[:, :])
                        mm.then_inc(t_done.sem, 1)

                def pv(b, u):
                    half = u % 2
                    pe.wait_ge(pt_ready.sem, pt_ready.have(b, 2 * u + 1))
                    pe.wait_ge(o_ready.sem, o_ready.back(b, u, 1))
                    for i in range(HH):
                        mm = nc.tensor.matmul(ob[:, i, :], PT[:, u % 2, i, :],
                                              vcur[:, 4 * (i // 2) + 2 * half + i % 2, :], start=True, stop=True)
                    mm.then_inc(pv_done.sem, 1)

                def misc_free(b, kind, t):
                    i = MISC.index((kind, t))
                    if i == 0:
                        pe.wait_ge(lg_out.sem, lg_out.back(b, QT - 1, QT))
                    else:
                        before, bt = MISC[i - 1]
                        c = {"o_turn": ot_ready, "out": x3_ready, "n_turn": n3T_ready, "router": lg_out}[before]
                        pe.wait_ge(c.sem, c.have(b, bt))

                def o_turn(b, t):
                    pe.wait_ge(o_ready.sem, o_ready.have(b, 2 * t + 1))
                    for c in range(DC):
                        mm = nc.tensor.transpose(misc[:, c * P:c * P + P], O[:, t % 2, c * P:c * P + P], k.ident[:, :])
                    mm.then_inc(ot_done.sem, 1)

                def out(b, t):
                    pe.wait_ge(ot_ready.sem, ot_ready.have(b, t))
                    for c in range(DC):
                        mm = nc.tensor.matmul(misc, OT[:, t % 2, c, :], wo[:, c, :], start=(c == 0), stop=(c == DC - 1))
                    mm.then_inc(wo_done.sem, 1)

                def n_turn(b, t):
                    pe.wait_ge(n3_ready.sem, n3_ready.have(b, t))
                    for c in range(DC):
                        mm = nc.tensor.transpose(misc[:, c * P:c * P + P], N3[:, t % 2, c * P:c * P + P], k.ident[:, :])
                    mm.then_inc(n3_read.sem, 1)

                def router(b, t):
                    pe.wait_ge(n3T_ready.sem, n3T_ready.have(b, t))
                    for c in range(DC):
                        mm = nc.tensor.matmul(misc[:, 0:E], N3T[:, t % 2, c, :], gw[:, c, :], start=(c == 0), stop=(c == DC - 1))
                    mm.then_inc(lg_done.sem, 1)

                def step(b, u):
                    if u == 0:
                        pe.wait_ge(qT_ready.sem, qT_ready.have(b, DC - 1))
                        pe.wait_ge(k_ready.sem, k_ready.have(b, 0))
                        pe.wait_ge(v_ready.sem, v_ready.have(b, 0))
                    if u < U1:
                        scores(b, u)
                    if 1 <= u <= U1:
                        turn(b, u - 1)
                    if 2 <= u <= U1 + 1:
                        pv(b, u - 2)
                    for f, (kind, lag) in zip((o_turn, out, n_turn, router), LAGS):
                        t = (u - lag) // 2
                        if (kind, t) in MISC and (u - lag) % 2 == 0:
                            misc_free(b, kind, t)
                            f(b, t)

                def body(b, prev, succ):
                    pe.wait_ge(p_ready.sem, p_ready.have(b, -1))
                    for t in range(QT):
                        pe.wait_ge(y_ready.sem, y_ready.have(b, t))
                        for c in range(DC):
                            mm = nc.tensor.transpose(bank[:, t, c * P:c * P + P], Y[:, t, c * P:c * P + P], k.ident[:, :])
                        mm.then_inc(y_read.sem, 1)

                    def queries(m):
                        if m == 0:
                            pe.wait_ge(xT_ready.sem, xT_ready.have(b, QT - 1))
                        for c in range(DC):
                            mm = nc.tensor.matmul(bank[:, m, :], wq[:, c, m * P:m * P + P], xT[:, c, :],
                                                  start=(c == 0), stop=(c == DC - 1))
                        mm.then_inc(q_done.sem, 1)
                    attend(b, prev, step, queries)

                def tail(b):
                    for u in range(U1, U1 + 8):
                        step(b, u)
                rounds(pe, body, tail)

            @block.scalar
            def _(act):
                credit(act, pt_ready)
                act.wait_ge(folded, 3)
                for n in range(2 * DC):
                    m, half = n // 2, n % 2
                    act.wait_ge(kv_done, n + 1)
                    act.activation(kT[:, m, half * 4 * CL:(half + 1) * 4 * CL], bank[:, n % 2, 0:4 * CL], ACT.Identity,
                                   bias=bk[:, m:m + 1]).then_inc(k_out, 1)
                act.wait_ge(k_out, 2 * DC)
                act.wait_ge(kzeroed, 1)

                def step(b, u):
                    if u < U1:
                        act.wait_ge(p_ready.sem, p_ready.have(b, u))
                        act.activation(Pr[:, u % 2, :, :], Pr[:, u % 2, :, :], ACT.Exp, scale=DH1 ** -0.5)\
                            .then_inc(exp_done.sem, 1)
                    if 1 <= u <= U1:
                        for q in range(2):
                            act.wait_ge(t_done.sem, t_done.have(b, 2 * (u - 1) + q))
                            if q == 0:
                                act.wait_ge(pv_done.sem, pv_done.back(b, u - 1, 2))
                            act.activation(PT[:, (u - 1) % 2, 4 * q:4 * q + 4, :],
                                           tb[q][0:CL, :].rearrange("p (h n) -> p h n", h=4), ACT.Copy)\
                                .then_inc(pt_ready.sem, 1)
                    if u >= 4 and (u - 4) % 2 == 0 and (u - 4) // 2 < QT:
                        t = (u - 4) // 2
                        act.wait_ge(ot_done.sem, ot_done.have(b, t))
                        act.wait_ge(wo_done.sem, wo_done.back(b, t, 2))
                        act.activation(OT[:, t % 2, :, :], misc.rearrange("p (c n) -> p c n", c=DC), ACT.Copy)\
                            .then_inc(ot_ready.sem, 1)
                    if u >= 8 and (u - 8) % 2 == 0 and (u - 8) // 2 < QT:
                        t = (u - 8) // 2
                        act.wait_ge(n3_read.sem, n3_read.have(b, t))
                        act.wait_ge(lg_done.sem, lg_done.back(b, t, 2))
                        act.activation(N3T[:, t % 2, :, :], misc.rearrange("p (c n) -> p c n", c=DC), ACT.Copy)\
                            .then_inc(n3T_ready.sem, 1)

                def body(b, prev, succ):
                    for t in range(QT):
                        act.wait_ge(y_read.sem, y_read.have(b, t))
                        act.activation(xT[:, :, t * P:t * P + P], bank[:, t, :].rearrange("p (c n) -> p c n", c=DC), ACT.Copy)\
                            .then_inc(xT_ready.sem, 1)
                    if prev:
                        act.wait_ge(s_done.sem, s_done.have(b, -1))
                    for i in range(4):
                        r = slice(DH1 * i, DH1 * i + DH1)
                        copy = act.activation(kcur[r, i::4, :], kT[r, :, ds(b * CL, CL)], ACT.Copy)
                    copy.then_inc(k_ready.sem, 1)

                    def queries(m):
                        act.wait_ge(q_done.sem, q_done.have(b, m))
                        act.activation(qT[:, m, :], bank[:, m, :], ACT.Identity, bias=bq[:, m:m + 1]).then_inc(qT_ready.sem, 1)
                    attend(b, prev, step, queries)

                def tail(b):
                    for u in range(U1, U1 + 8):
                        step(b, u)
                rounds(act, body, tail)

            @block.vector
            def _(dve):
                credit(dve, x2_ready, p_ready, o_ready, lg_out, n3_ready)
                dve.wait_ge(folded, 3)
                for b in range(B):
                    dve.wait_ge(kv_done, 2 * DC + b + 1)
                    dve.tensor_tensor(V[:, b, :, 0:DH1], bank[0:CL, 2 + b % 2, :].rearrange("p (h d) -> p h d", h=H1),
                                      bv[0:CL, :].rearrange("p (h d) -> p h d", h=H1), ALU.add).then_inc(v_out, 1)

                def prep_a(b, t, comb):
                    s = t % 2
                    dve.wait_ge(x_biased.sem, x_biased.have(b, t))
                    if comb:
                        for c in range(2):
                            dve.wait_ge(g_in[s][c], b * 32 + 16 * (t // 2 + 1))
                        dve.scalar_tensor_tensor(X[:, t, :], G[:, s, 0, :], wcol[:, s, 0:1], X[:, t, :], ALU.mult, ALU.add)\
                            .then_inc(summed.sem, 1)
                        dve.wait_ge(summed.sem, summed.have(b, t))
                        dve.scalar_tensor_tensor(X[:, t, :], G[:, s, 1, :], wcol[:, s, 1:2], X[:, t, :], ALU.mult, ALU.add)\
                            .then_inc(x2_ready.sem, 1)
                        dve.wait_ge(x2_ready.sem, x2_ready.have(b, t))
                    else:
                        dve.sem_inc(x2_ready.sem, 1)
                    dve.bn_stats(bst[:, t, :], X[:, t, :]).then_inc(bn_step.sem, 1)
                    dve.wait_ge(bn_step.sem, bn_step.have(b, t))
                    dve.nop(nofuse=True)
                    dve.bn_aggr(mv[:, t, :], bst[:, t, :]).then_inc(stat.sem, 1)

                def prep_b(b, t):
                    dve.wait_ge(rst.sem, rst.have(b, t))
                    dve.wait_ge(y_read.sem, y_read.back(b, t, QT))
                    dve.tensor_scalar(Y[:, t, :], X[:, t, :], mv[:, t, 0:1], rstd[:, t:t + 1], ALU.subtract, ALU.mult)\
                        .then_inc(y_ready.sem, 1)

                for t in range(QT):
                    prep_a(0, t, True)
                    prep_b(0, t)

                def step(b, u):
                    if u < U1:
                        s = u % 2
                        dve.wait_ge(s_done.sem, s_done.have(b, u))
                        dve.tensor_reduce(smax[:, s, :].rearrange("p (r c) -> p r c", r=2), Sb[s], AX.X, ALU.max)\
                            .then_inc(max_done.sem, 1)
                        dve.wait_ge(max_done.sem, max_done.have(b, u))
                        dve.wait_ge(t_done.sem, t_done.back(b, 2 * u + 1, 4))
                        dve.tensor_tensor(Pr[:, s, :, :].rearrange("p (r c) n -> p r c n", r=2), Sb[s],
                                          smax[:, s, :].rearrange("p (r c) -> p r c", r=2).unsqueeze(3)
                                          .to_broadcast([P, 2, 4, CL]), ALU.subtract).then_inc(p_ready.sem, 1)
                    if 2 <= u <= U1 + 1:
                        v = u - 2
                        dve.wait_ge(pv_done.sem, pv_done.have(b, v))
                        dve.wait_ge(ot_done.sem, ot_done.back(b, v // 2, 2))
                        dve.reciprocal(rinv[:, v % 2, :], ob[:, :, DH1]).then_inc(rinv_step.sem, 1)
                        dve.wait_ge(rinv_step.sem, rinv_step.have(b, v))
                        half = v % 2
                        dve.tensor_tensor(O[:, (v // 2) % 2, :].rearrange("p (c r d) -> p c r d", c=4, r=4)
                                          [:, :, 2 * half:2 * half + 2, :],
                                          ob[:, :, 0:DH1].rearrange("p (c r) d -> p c r d", r=2),
                                          rinv[:, half, :].rearrange("p (c r) -> p c r", r=2).unsqueeze(3)
                                          .to_broadcast([P, 4, 2, DH1]), ALU.mult).then_inc(o_ready.sem, 1)
                    if u >= 5 and (u - 5) % 2 == 0 and (u - 5) // 2 < QT:
                        t = (u - 5) // 2
                        dve.wait_ge(wo_done.sem, wo_done.have(b, t))
                        dve.wait_ge(r_biased.sem, r_biased.have(b, t))
                        dve.scalar_tensor_tensor(R[:, t, :], misc, k.gate[:, 1:2], R[:, t, :], ALU.mult, ALU.add)\
                            .then_inc(x3_ready.sem, 1)
                        dve.wait_ge(x3_ready.sem, x3_ready.have(b, t))
                        dve.bn_stats(bst3[:, t, :], R[:, t, :]).then_inc(bn3_step.sem, 1)
                        dve.wait_ge(bn3_step.sem, bn3_step.have(b, t))
                        dve.nop(nofuse=True)
                        dve.bn_aggr(mv3[:, t, :], bst3[:, t, :]).then_inc(stat3.sem, 1)
                    if u >= 7 and (u - 7) % 2 == 0 and (u - 7) // 2 < QT:
                        t = (u - 7) // 2
                        dve.wait_ge(rst3.sem, rst3.have(b, t))
                        dve.wait_ge(n3_read.sem, n3_read.back(b, t, 2))
                        dve.tensor_scalar(N3[:, t % 2, :], R[:, t, :], mv3[:, t, 0:1], rstd3[:, t:t + 1],
                                          ALU.subtract, ALU.mult).then_inc(n3_ready.sem, 1)
                    if u >= 9 and (u - 9) % 2 == 0 and (u - 9) // 2 < QT:
                        t = (u - 9) // 2
                        dve.wait_ge(lg_done.sem, lg_done.have(b, t))
                        dve.tensor_copy(k.logits[:, ds(b * QT + t, 1), :].rearrange("p o e -> p (o e)"), misc[:, 0:E])\
                            .then_inc(lg_out.sem, 1)

                def body(b, prev, succ):
                    def with_prep(bb, u):
                        step(bb, u)
                        if bb is b and succ is not None:
                            (prep_a(b + 1, u // 2, succ) if u % 2 == 0 else prep_b(b + 1, u // 2))
                    attend(b, prev, with_prep, lambda m: None)

                def tail(b):
                    for u in range(U1, U1 + 8):
                        step(b, u)
                rounds(dve, body, tail)


def combine(nc, k, out):
    RING = 4
    NT = B * QT
    with ExitStack() as ctx:
        sb = lambda n, s, d=F32: ctx.enter_context(nc.sbuf_tensor("c_" + n, s, d))
        sem = lambda n: k.sems.enter_context(nc.semaphore("c_" + n))
        count = lambda n, per, credit=0: Count(k.sems, nc, "c_" + n, per, credit)
        X, G = sb("X", [P, RING, D]), sb("G", [P, RING, 2, D])
        icol, wcol = sb("icol", [P, RING, 2], I32), sb("wcol", [P, RING, 2])
        x_in, x_out = [sem(f"x_in{q}") for q in range(RING)], [sem(f"x_out{q}") for q in range(RING)]
        g_in = [[sem(f"g_in{q}{c}") for c in range(2)] for q in range(RING)]
        icopied, half, done = count("icopied", RING), count("half", RING), count("done", RING, RING)
        with nc.Block() as block:
            @block.sync
            def _(sp):
                with sp.Fori(0, NT // RING) as i:
                    for q in range(RING):
                        sp.wait_ge(x_out[q], i * 16 + 16)
                        sp.dma_start(X[:, q, :], k.x3[ds((i * RING + q) * P, P), :]).then_inc(x_in[q], 16)

            @block.gpsimd
            def _(pool):
                with pool.Fori(0, NT // RING) as i:
                    for q in range(RING):
                        pool.wait_ge(done.sem, done.back(i, q, RING))
                        for c in range(2):
                            pool.tensor_copy(icol[:, q, c:c + 1], k.slot1[:, ds(i * RING + (q + c * NT), 1)])
                            last = pool.tensor_copy(wcol[:, q, c:c + 1], k.w1[:, ds(i * RING + (q + c * NT), 1)])
                        last.then_inc(icopied.sem, 1)
                        pool.wait_ge(icopied.sem, icopied.have(i, q))
                        pool.nop(nofuse=True)
                        for c in range(2):
                            pool.indirect_dma_start(G[:, q, c, :], None, k.y1, bass.IndirectOffsetOnAxis(icol[:, q, c:c + 1], 0))\
                                .then_inc(g_in[q][c], 16)

            @block.vector
            def _(dve):
                dve.sem_inc(done.sem, done.credit)
                with dve.Fori(0, NT // RING) as i:
                    for q in range(RING):
                        dve.wait_ge(x_in[q], i * 16 + 16)
                        dve.wait_ge(g_in[q][0], i * 16 + 16)
                        dve.scalar_tensor_tensor(X[:, q, :], G[:, q, 0, :], wcol[:, q, 0:1], X[:, q, :], ALU.mult, ALU.add)\
                            .then_inc(half.sem, 1)
                        dve.wait_ge(half.sem, half.have(i, q))
                        dve.wait_ge(g_in[q][1], i * 16 + 16)
                        dve.scalar_tensor_tensor(X[:, q, :], G[:, q, 1, :], wcol[:, q, 1:2], X[:, q, :], ALU.mult, ALU.add)\
                            .then_inc(done.sem, 1)

            @block.scalar
            def _(act):
                for q in range(RING):
                    act.sem_inc(x_out[q], 16)
                with act.Fori(0, NT // RING) as i:
                    for q in range(RING):
                        act.wait_ge(done.sem, done.have(i, q))
                        act.dma_start(out[ds((i * RING + q) * P, P), :], X[:, q, :]).then_inc(x_out[q], 16)
                for q in range(RING):
                    act.wait_ge(x_out[q], 16 * (NT // RING + 1))


INS = ["x", "ctx", "mask", "g_xattn", "g_ffn", "wqT", "wlkvT", "wkvT", "woT", "lng", "lnb", "lxg", "lxb",
       "qng", "kng", "bo0", "ei", "ew", "w1_0", "w2_0", "bf0", "wq1", "wk1", "wv1", "wo1", "bq1", "bk1", "bv1", "bo1",
       "gw1", "ctxT", "w1_1", "w2_1", "w3_1"]


def build(nc, ins, out):
    k = Core()
    with ExitStack() as ctx:
        k.sems = ctx
        sb = lambda n, s, d=F32: ctx.enter_context(nc.sbuf_tensor(n, s, d))
        k.ident, k.tri, k.ones = sb("ident", [P, P]), sb("tri", [P, P]), sb("ones", [P, P])
        k.halfneg, k.gate = sb("halfneg", [P, 16]), sb("gate", [P, 4])
        k.iota_e, k.iota_p, k.tokcol = sb("iota_e", [P, E]), sb("iota_p", [P, P]), sb("tokcol", [P, B * QT])
        k.bank = ctx.enter_context(nc.psum_tensor("bank", [P, 8, 512], F32))
        k.slot0, k.slot1 = sb("slot0", [P, NA0], I32), sb("slot1", [P, NA1], I32)
        k.idx0, k.idx1 = sb("idx0", [P, NT0 * ROWS // P], I32), sb("idx1", [P, NT1 * ROWS // P], I32)
        k.te0, k.te1 = sb("te0", [1, NT0], I32), sb("te1", [1, NT1], I32)
        k.w0, k.w1 = sb("w0", [P, NA0]), sb("w1", [P, NA1])
        k.logits = sb("logits", [P, B * QT, E])
        dram = lambda n, rows: nc.dram_tensor(n, [rows, D], F32, kind="Internal").ap()
        k.x1, k.x2, k.x3 = dram("x1", NTOK), dram("x2", NTOK), dram("x3", NTOK)
        k.y0, k.y1 = dram("y0", NT0 * ROWS), dram("y1", NT1 * ROWS)
        setup(nc, k, ins)
        attention0(nc, k, ins)
        route_given(nc, k, ins)
        experts(nc, k, "e0_", k.x1, ins["w1_0"], None, ins["w2_0"], FF0, NT0, k.idx0, k.te0, k.y0)
        attention1(nc, k, ins)
        route_top2(nc, k)
        experts(nc, k, "e1_", k.x3, ins["w1_1"], ins["w3_1"], ins["w2_1"], FF1, NT1, k.idx1, k.te1, k.y1)
        combine(nc, k, out)


def kernel(**inputs):
    import numpy as np
    import concourse.bacc as bacc
    from concourse.bass_utils import run_bass_kernel_spmd

    columns = lambda v: v.reshape(-1, P).T
    assigned = lambda v: v.reshape(-1, P, 2).transpose(1, 2, 0).reshape(P, -1)
    a = {n: np.asarray(v) for n, v in inputs.items()}
    host = {
        "x": a["x"].reshape(NTOK, D), "ctx": a["ctx_768"].reshape(B * CL, CD),
        "mask": a["mask_BxS2_bk0"], "g_xattn": a["g_xattn"], "g_ffn": a["g_ffn"],
        "wqT": a["L0_xattn_Wq"].T, "wlkvT": a["L0_xattn_Wlkv"].T, "wkvT": a["L0_xattn_Wkv"].T,
        "woT": a["L0_xattn_Wo"].T, "lng": columns(a["L0_xattn_ln_l_g"]), "lnb": columns(a["L0_xattn_ln_l_b"]),
        "lxg": columns(a["L0_xattn_ln_x_g"]), "lxb": columns(a["L0_xattn_ln_x_b"]), "qng": a["L0_xattn_qn_g"],
        "kng": a["L0_xattn_kn_g"], "bo0": a["L0_xattn_bo"],
        "ei": assigned(a["L0_ffn_expert_indices"]), "ew": assigned(a["L0_ffn_expert_weights"]),
        "w1_0": a["L0_ffn_w1"], "w2_0": a["L0_ffn_w2"], "bf0": a["L0_ffn_bias"],
        "wq1": a["L1_xattn_wq"], "wk1": a["L1_xattn_wk"], "wv1": a["L1_xattn_wv"], "wo1": a["L1_xattn_wo"],
        "bq1": columns(a["L1_xattn_bq"]), "bk1": columns(a["L1_xattn_bk"]), "bv1": a["L1_xattn_bv"],
        "bo1": a["L1_xattn_bo"], "gw1": a["L1_ffn_gate_w"].T, "ctxT": a["ctx_768"].reshape(B * CL, CD).T,
        "w1_1": a["L1_ffn_w1"], "w2_1": a["L1_ffn_w2"], "w3_1": a["L1_ffn_w3"],
    }
    nc = bacc.Bacc("TRN2", target_bir_lowering=False, num_devices=1)
    arrays, ins = {}, {}
    for name in INS:
        v = np.ascontiguousarray(host[name])
        arrays["in_" + name] = v
        ins[name] = nc.dram_tensor("in_" + name, v.shape, mybir.dt.from_np(v.dtype), kind="ExternalInput").ap()
    out = nc.dram_tensor("out_0", (NTOK, D), F32, kind="ExternalOutput").ap()
    build(nc, ins, out)
    r = run_bass_kernel_spmd(nc, [arrays], core_ids=[0])
    return r.results[0]["out_0"].reshape(B, S, D)
```
